# Optimizing a Trainium2 kernel written in Bass

```python
import numpy as np
import jax
import jax.numpy as jnp

def _softmax(x, axis=-1):
    return jax.nn.softmax(x, axis=axis)
def _gelu(x):
    return jax.nn.gelu(x, approximate=True)
def _silu(x):
    return jax.nn.silu(x)
def _sigmoid(x):
    return jax.nn.sigmoid(x)
def _layernorm(x, axis=-1, eps=1e-5):
    m = jnp.mean(x, axis=axis, keepdims=True)
    v = jnp.var(x, axis=axis, keepdims=True)
    return (x - m) / jnp.sqrt(v + eps)
def _scatter_add(tgt, idx, src, axis=0):
    return tgt.at[idx].add(src)
def _segment_sum(src, seg, n):
    return jax.ops.segment_sum(src, seg, n)

kernel_name = 'mk_conv_seq_d1_conv_nchw256_4bc06a'

def setup_inputs(seed: int = 0):
    np.random.seed(seed)
    _w = jnp.asarray
    def _rec_inputs():
        import jax
        import jax.numpy as jnp
        _gk = jax.random.key(seed)
        x = 7.22e-05 + 1 * jax.random.normal(jax.random.fold_in(_gk, 1), (32, 256, 32, 32), jnp.float32)
        return x
    x = _rec_inputs()
    def _L0_conv_setup():
        import jax, jax.numpy as jnp
        import numpy as np
        T_FRAME = 8
        BN_EPS = 1e-05

        def _conv1x1(x_flat, w, b):
            return jnp.einsum('oc,ncp->nop', w, x_flat) + b[None, :, None]
        key = jax.random.key(seed)
        ks = jax.random.split(key, 9)
        N, C, H, W = (32, 256, 32, 32)
        scale = 1.0 / np.sqrt(C)
        return {'x': jax.random.normal(ks[0], (N, C, H, W), dtype=jnp.float32), 'w1': jax.random.normal(ks[1], (C, C), dtype=jnp.float32) * scale, 'b1': jax.random.normal(ks[2], (C,), dtype=jnp.float32) * 0.01, 'w2': jax.random.normal(ks[3], (C, C), dtype=jnp.float32) * scale, 'b2': jax.random.normal(ks[4], (C,), dtype=jnp.float32) * 0.01, 'w0': jax.random.normal(ks[5], (C, C), dtype=jnp.float32) * scale, 'b0': jax.random.normal(ks[6], (C,), dtype=jnp.float32) * 0.01, 'gamma': jax.random.normal(ks[7], (C,), dtype=jnp.float32) * 0.1 + 1.0, 'beta': jax.random.normal(ks[8], (C,), dtype=jnp.float32) * 0.01}
    _L0_conv_all = _L0_conv_setup()
    _L0_conv_in = {k: v for k, v in _L0_conv_all.items() if k in ('w1', 'b1', 'w2', 'b2', 'w0', 'b0', 'gamma', 'beta', )}
    del _L0_conv_all

    return {
        "x": x,
        "L0_conv_w1": _L0_conv_in["w1"],
        "L0_conv_b1": _L0_conv_in["b1"],
        "L0_conv_w2": _L0_conv_in["w2"],
        "L0_conv_b2": _L0_conv_in["b2"],
        "L0_conv_w0": _L0_conv_in["w0"],
        "L0_conv_b0": _L0_conv_in["b0"],
        "L0_conv_gamma": _L0_conv_in["gamma"],
        "L0_conv_beta": _L0_conv_in["beta"],
    }

def reference(x, L0_conv_w1, L0_conv_b1, L0_conv_w2, L0_conv_b2, L0_conv_w0, L0_conv_b0, L0_conv_gamma, L0_conv_beta):
    import jax
    import jax.numpy as jnp
    def _L0_conv_ref(x, w1, b1, w2, b2, w0, b0, gamma, beta):
        import jax, jax.numpy as jnp
        import numpy as np
        T_FRAME = 8
        BN_EPS = 1e-05

        def _conv1x1(x_flat, w, b):
            return jnp.einsum('oc,ncp->nop', w, x_flat) + b[None, :, None]
        N, C, H, W = x.shape
        T = T_FRAME
        V = N // T
        xv = x.reshape(V, T, C, H, W)
        x1 = jnp.concatenate([xv[:, :1], xv[:, :-1]], axis=1)
        x2 = jnp.concatenate([x1[:, :1], x1[:, :-1]], axis=1)
        HW = H * W
        xf = x.reshape(N, C, HW)
        x1f = x1.reshape(N, C, HW)
        x2f = x2.reshape(N, C, HW)
        phi1 = _conv1x1(x1f, w1, b1)
        phi2 = _conv1x1(x2f, w2, b2)
        phi0 = _conv1x1(xf, w0, b0)
        scores = jnp.einsum('nca,ncb->nab', phi1, phi2) * C ** (-0.5)
        attn = jax.nn.softmax(scores, axis=2)
        out = jnp.einsum('ntg,ncg->nct', attn, phi0)
        out = out.reshape(N, C, H, W)
        mean = jnp.mean(out, axis=(0, 2, 3), keepdims=True)
        var = jnp.var(out, axis=(0, 2, 3), keepdims=True)
        out = (out - mean) * jax.lax.rsqrt(var + BN_EPS)
        out = out * gamma[None, :, None, None] + beta[None, :, None, None]
        return x + out

    def _gn(v, G=32, eps=1e-5):
        B_, C_, H_, W_ = v.shape
        g = v.reshape(B_, G, C_ // G, H_, W_)
        m = jnp.mean(g, axis=(2, 3, 4), keepdims=True)
        s = jnp.var(g, axis=(2, 3, 4), keepdims=True)
        return ((g - m) / jnp.sqrt(s + eps)).reshape(v.shape)

    def _ln_c(v, eps=1e-6):
        m = jnp.mean(v, axis=1, keepdims=True)
        s = jnp.var(v, axis=1, keepdims=True)
        return (v - m) / jnp.sqrt(s + eps)

    def _ln_t(v, eps=1e-5):
        m = jnp.mean(v, axis=-1, keepdims=True)
        s = jnp.var(v, axis=-1, keepdims=True)
        return (v - m) / jnp.sqrt(s + eps)

    def _to_tokens(v):
        B_, C_, H_, W_ = v.shape
        return v.reshape(B_, C_, H_ * W_).transpose(0, 2, 1)
    def _from_tokens(t, like):
        B_, C_, H_, W_ = like.shape
        return t.transpose(0, 2, 1).reshape(B_, C_, H_, W_)

    x = _L0_conv_ref(x, L0_conv_w1, L0_conv_b1, L0_conv_w2, L0_conv_b2, L0_conv_w0, L0_conv_b0, L0_conv_gamma, L0_conv_beta)
    return x


_drawn_inputs = setup_inputs


def setup_inputs(seed=0):
    import zlib

    import numpy as np

    out = dict(_drawn_inputs(seed))
    spreads = {}
    factors = {'L0_conv_b1': 8.0, 'L0_conv_b2': 8.0, 'L0_conv_b0': 8.0, 'L0_conv_beta': 8.0}
    for name, (base, spread) in spreads.items():
        noise = np.random.default_rng([zlib.crc32(name.encode()), seed]).standard_normal(out[name].shape)
        drawn = base * np.exp(spread * noise) if base else spread * noise
        out[name] = jnp.asarray(drawn.astype(out[name].dtype))
    for name, factor in factors.items():
        out[name] = (out[name] * factor).astype(out[name].dtype)
    return out
```

```python
from contextlib import ExitStack

import concourse.bass as bass
from concourse import mybir
from concourse.alu_op_type import AluOpType as ALU

ACT = mybir.ActivationFunctionType
F32 = mybir.dt.float32
F32R = mybir.dt.float32r
AX_X = mybir.AxisListType.X

P = 128
T = 8
EPS = 1e-5
STEPS = T - 1
STRIPS = 8
SLOTS = STEPS * STRIPS
LAG = 5
HEAD = 9
XRING = 3
STAGES = 4

N_STRIP = SLOTS
N_Z = 2 * STEPS
N_VAL = 4 * T
N_SPLIT = 2 * T
N_OUT = 4 * T


def nth(v, per_video, index):
    return v * per_video + (index + 1)


def units_of_slot(k):
    units = [("scores", k)]
    step, strip = divmod(k, STRIPS)
    if strip == STRIPS - 1:
        units += [("z", 2 * (step + 1) + m) for m in range(2)]
    if strip == 4:
        units += [("values", 4 * (step + 1) + j) for j in range(4)]
    if k == SLOTS - 2:
        units += [("values", N_VAL + j) for j in range(4)]
    return units


UNITS = [u for k in range(SLOTS) for u in units_of_slot(k)]
assert len(UNITS) % 2 == 0
BUFFER = {u: n % 2 for n, u in enumerate(UNITS)}
BUFFER |= {("values", j): BUFFER["values", N_VAL + j] for j in range(4)}
BUFFER |= {("z", m): BUFFER["z", N_Z + m] for m in range(2)}


def before_in_buffer(unit, last):
    n = UNITS.index(unit) - 2
    while last and UNITS[n][0] == "values" and UNITS[n][1] >= N_VAL:
        n -= 2
    kind, index = UNITS[n]
    return (kind, index) if n >= 0 else (kind, index - {"scores": N_STRIP, "z": N_Z, "values": N_VAL}[kind])


def out_quarter(k):
    step, eighth = divmod(k - LAG, STRIPS)
    return step, eighth // 4, eighth % 4 // 2, eighth % 2 == 1


def out_tiles(k):
    step, half, m, _ = out_quarter(k)
    if step == 0:
        return [(f, 4 * half + 2 * m + f) for f in range(2)]
    if step > 0:
        return [(step + 1, 4 * (step + 1) + 2 * half + m)]
    return [(T - 1, 4 * (T - 1) + 2 * half + m - N_OUT)]


def conv_attention_norm(nc, x, w1, b1, w2, b2, w0, b0, gamma, beta, out):
    N, C, H, W = x.shape
    HW = H * W
    VIDEOS = N // T
    assert C == 2 * P and HW == STRIPS * P and N % T == 0
    SCALE = float(C) ** -0.5
    CW = C + 2
    HALF = HW // 2

    x_d = x.rearrange("n (c p) h w -> n p c (h w)", p=P)
    out_d = out.rearrange("n (c p) h w -> n p c (h w)", p=P)
    attended_d = nc.dram_tensor("attended", (N, P, 2, HW), F32, kind="Internal").ap()

    with ExitStack() as ctx:
        def sem(name):
            return ctx.enter_context(nc.semaphore(name))

        def sb(name, shape, dt, stack=ctx):
            return stack.enter_context(nc.sbuf_tensor(name, shape, dt))

        stats = sb("stats", [P, 2, 2 * N, 6], F32)
        gamma_c = sb("gamma_c", [P, 2], F32)
        beta_c = sb("beta_c", [P, 2], F32)

        weights_loaded = sem("weights_loaded")
        ident_zero = sem("ident_zero")
        ident_ready = sem("ident_ready")
        prep_mm = sem("prep_mm")
        prep_hi = sem("prep_hi")
        prep_ready = sem("prep_ready")
        x_loaded = sem("x_loaded")
        x_hi = sem("x_hi")
        x_split = sem("x_split")
        scores_done = sem("scores_done")
        max_done = sem("max_done")
        shift_done = sem("shift_done")
        exp_done = sem("exp_done")
        recip_done = sem("recip_done")
        probs_done = sem("probs_done")
        turned = sem("turned")
        turned_hi = sem("turned_hi")
        turned_split = sem("turned_split")
        z_done = sem("z_done")
        z_hi = sem("z_hi")
        z_split = sem("z_split")
        values_done = sem("values_done")
        values_added = sem("values_added")
        values_hi = sem("values_hi")
        values_split = sem("values_split")
        out_done = sem("out_done")
        out_copied = sem("out_copied")
        stats_done = sem("stats_done")
        out_stored = [sem(f"out_stored{i}") for i in range(STAGES)]

        with ExitStack() as one:
            def pb(name, shape):
                return one.enter_context(nc.psum_tensor(name, shape, F32))

            raw = sb("raw", [P, 2, HW], F32, one)
            xh = sb("xh", [P, XRING, 2, HW], F32R, one)
            xl = sb("xl", [P, XRING, 2, HW], F32R, one)
            zh = sb("zh", [P, 2, HW], F32R, one)
            zl = sb("zl", [P, 2, HW], F32R, one)
            vh = sb("vh", [P, 2, STRIPS, C], F32R, one)
            vl = sb("vl", [P, 2, STRIPS, C], F32R, one)
            ph = sb("ph", [P, 2, STRIPS, HALF], F32R, one)
            pl = sb("pl", [P, 2, STRIPS, HALF], F32R, one)
            probs = sb("probs", [P, 2, HW], F32, one)
            vsum = sb("vsum", [P, 2, 2, CW], F32, one)
            stage = sb("stage", [P, STAGES, HALF], F32, one)
            mh = sb("mh", [P, 2, C], F32R, one)
            ml = sb("ml", [P, 2, C], F32R, one)
            wvh = sb("wvh", [P, 2, CW], F32R, one)
            wvl = sb("wvl", [P, 2, CW], F32R, one)
            vbias = sb("vbias", [P, 2, CW], F32, one)
            u_c = sb("u_c", [P, 2], F32, one)
            b1_c = sb("b1_c", [P, 2], F32, one)
            b2_c = sb("b2_c", [P, 2], F32, one)
            ident = sb("ident", [P, P], F32, one)
            r_all = sb("r_all", [P, T, STRIPS], F32, one)
            negmax = sb("negmax", [P, 2], F32, one)
            shift = sb("shift", [P, 2], F32, one)
            total = sb("total", [P, 2], F32, one)
            inverse = sb("inverse", [P, 2], F32, one)

            sp = [pb(f"sp{i}", [P, 2, HALF]) for i in range(2)]
            tp = pb("tp", [P, STRIPS, P])
            op = [pb(f"op{i}", [P, HALF]) for i in range(2)]

            w1_s = probs[:, 0, 0:2 * C].rearrange("p (t c) -> p t c", t=2)
            w2_s = probs[:, 0, 2 * C:4 * C].rearrange("p (t c) -> p t c", t=2)
            w0_s = probs[:, 1, 0:2 * C].rearrange("p (t c) -> p t c", t=2)

            def span(a, b):
                return slice(a * P, b * P)

            with nc.Block() as block:

                @block.gpsimd
                def _(pool):
                    nc.gpsimd.memset(ident[:], 0.0).then_inc(ident_zero, 1)
                    pool.wait_ge(ident_zero, 1)
                    nc.gpsimd.affine_select(out=ident[:], in_=ident[:], compare_op=ALU.not_equal, fill=1.0,
                                            base=0, pattern=[[-1, P]], channel_multiplier=1).then_inc(ident_ready, 1)

                @block.sync
                def _(sp_):
                    for dst, src in ((w1_s, w1), (w2_s, w2), (w0_s, w0)):
                        sp_.dma_start(dst, src.rearrange("(t p) c -> p t c", p=P)).then_inc(weights_loaded, 16)
                    with nc.allow_non_contiguous_dma(reason="five columns of 256 numbers"):
                        for dst, src in ((b1_c, b1), (b2_c, b2), (gamma_c, gamma), (beta_c, beta)):
                            sp_.dma_start(dst[:], src.rearrange("(t p) -> p t", p=P)).then_inc(weights_loaded, 16)
                    for j in range(2):
                        sp_.dma_start(vbias[:, j, 0:C], b0.partition_broadcast(P)).then_inc(weights_loaded, 16)
                    sp_.dma_start(raw[:], x_d[0]).then_inc(x_loaded, 16)
                    sp_.wait_ge(x_split, 2)
                    sp_.dma_start(raw[:], x_d[1]).then_inc(x_loaded, 16)

                    def slot(v, k, first=False, last=False, tail=False):
                        step, strip = divmod(k, STRIPS)
                        load = step + 2 if strip == 2 else T + 1 if k == SLOTS - 2 else None
                        if load is not None and not tail and not (last and load >= T):
                            sp_.wait_ge(x_split, nth(v, N_SPLIT, 2 * load - 1))
                            sp_.dma_start(raw[:], x_d[v * T + load]).then_inc(x_loaded, 16)
                        _, half, m, second = out_quarter(k)
                        if second and not (first and k < LAG):
                            for frame, tile in out_tiles(k):
                                n = v * T + (frame if tile >= 0 else frame - T)
                                sp_.wait_ge(out_copied, nth(v, N_OUT, tile))
                                sp_.dma_start(attended_d[n][:, m, half * HALF:(half + 1) * HALF],
                                              stage[:, tile % STAGES, :]).then_inc(out_stored[tile % STAGES], 16)

                    for k in range(HEAD):
                        slot(0, k, first=True)
                    with sp_.Fori(0, VIDEOS - 1) as v:
                        for k in range(HEAD, SLOTS):
                            slot(v, k)
                        for k in range(HEAD):
                            slot(v + 1, k)
                    for k in range(HEAD, SLOTS):
                        slot(VIDEOS - 1, k, last=True)
                    for k in range(LAG):
                        slot(VIDEOS, k, tail=True)
                    for s in out_stored:
                        sp_.wait_ge(s, 16 * VIDEOS * N_OUT // STAGES)

                @block.tensor
                def _(pe):
                    def product(outs, weights, movings, start=True, stop=True):
                        n = len(weights)
                        for c, (w_hi, w_lo) in enumerate(weights):
                            for w, part in ((w_hi, 0), (w_hi, 1), (w_lo, 0)):
                                for h, o in enumerate(outs):
                                    mm = nc.tensor.matmul(o, w, movings[c][h][part],
                                                          start=start and c == 0 and part == 0 and w is w_hi,
                                                          stop=stop and c == n - 1 and w is w_lo)
                        return mm

                    pe.wait_ge(weights_loaded, 16 * 9)
                    pe.wait_ge(ident_ready, 1)
                    for i in range(2):
                        for o in range(2):
                            nc.tensor.matmul(sp[0][:, i, 0:C], w1_s[:, o, span(i, i + 1)], w2_s[:, o, :],
                                             start=o == 0, stop=o == 1)
                    for i in range(2):
                        for o in range(2):
                            nc.tensor.transpose(sp[1][:, i, span(o, o + 1)], w0_s[:, o, span(i, i + 1)], ident[:])
                    for at, (w, b) in enumerate(((w2_s, b1_c), (w1_s, b2_c))):
                        for m in range(2):
                            for o in range(2):
                                nc.tensor.matmul(op[0][:, 2 * at + m:2 * at + m + 1], w[:, o, span(m, m + 1)],
                                                 b[:, o:o + 1], start=o == 0, stop=o == 1)
                    for o in range(2):
                        mm = nc.tensor.matmul(op[0][:, 4:5], b1_c[:, o:o + 1].to_broadcast([P, P]),
                                              b2_c[:, o:o + 1], start=o == 0, stop=o == 1)
                    mm.then_inc(prep_mm, 1)

                    def wait_buffer(v, unit, last=False):
                        kind, index = before_in_buffer(unit, last)
                        if kind == "scores":
                            if not (isinstance(v, int) and nth(v, N_STRIP, index) <= 0):
                                pe.wait_ge(exp_done, nth(v, N_STRIP, index))
                        elif kind == "z":
                            pe.wait_ge(z_split, nth(v, N_Z, index))
                        else:
                            pe.wait_ge(values_added, nth(v, N_VAL, index))

                    def scores(v, k, last):
                        step, strip = divmod(k, STRIPS)
                        key = max(step - 1, 0) % XRING
                        wait_buffer(v, ("scores", k), last)
                        if strip == 0:
                            pe.wait_ge(z_split, nth(v, N_Z, 2 * step + 1))
                        a = span(strip, strip + 1)
                        halves = [slice(h * HALF, (h + 1) * HALF) for h in range(2)]
                        product([sp[BUFFER["scores", k]][:, h, :] for h in range(2)],
                                [(zh[:, c, a], zl[:, c, a]) for c in range(2)],
                                [[(xh[:, key, c, s], xl[:, key, c, s]) for s in halves] for c in range(2)]
                                ).then_inc(scores_done, 1)

                    def make_z(v, frame):
                        for m in range(2):
                            index = 2 * frame + m
                            q = frame % STEPS % XRING
                            if index >= 2:
                                wait_buffer(v, ("z", index))
                            else:
                                pe.wait_ge(values_added, 4 - m)
                            pe.wait_ge(x_split, nth(v, N_SPLIT, 2 * (frame if frame < STEPS else T) + 1))
                            halves = [slice(h * HALF, (h + 1) * HALF) for h in range(2)]
                            product([sp[BUFFER["z", index]][:, h, :] for h in range(2)],
                                    [(mh[:, c, span(m, m + 1)], ml[:, c, span(m, m + 1)]) for c in range(2)],
                                    [[(xh[:, q, c, s], xl[:, q, c, s]) for s in halves] for c in range(2)]
                                    ).then_inc(z_done, 1)

                    def make_values(v, frame):
                        q = frame % T % XRING
                        for j in range(4):
                            index = 4 * frame + j
                            if index >= 4:
                                wait_buffer(v, ("values", index))
                            elif j >= 2:
                                pe.wait_ge(values_added, j - 1)
                            else:
                                pe.wait_ge(prep_ready, 1)
                            pe.wait_ge(x_split, nth(v, N_SPLIT, 2 * frame + 1))
                            for i in range(2):
                                a = span(2 * j + i, 2 * j + i + 1)
                                mm = product([sp[BUFFER["values", index]][:, i, 0:CW]],
                                             [(xh[:, q, c, a], xl[:, q, c, a]) for c in range(2)],
                                             [[(wvh[:, c, :], wvl[:, c, :])] for c in range(2)])
                            mm.then_inc(values_done, 1)

                    def turn(v, k):
                        pe.wait_ge(probs_done, nth(v, N_STRIP, k))
                        if not (isinstance(v, int) and nth(v, N_STRIP, k - 1) <= 0):
                            pe.wait_ge(turned_split, nth(v, N_STRIP, k - 1))
                        for j in range(STRIPS):
                            tr = nc.tensor.transpose(tp[:, j, :], probs[:, k % 2, span(j, j + 1)], ident[:])
                        tr.then_inc(turned, 1)

                    def attend(v, k):
                        step, half, m, second = out_quarter(k)
                        for frame, tile in out_tiles(k):
                            if not second:
                                if m == 0:
                                    pe.wait_ge(turned_split, nth(v, N_STRIP, STRIPS * step + 4 * half + 3))
                                    pe.wait_ge(values_split, nth(v, N_VAL, 4 * (step + 1) + 3 if step >= 0 else -1))
                                if not (isinstance(v, int) and nth(v, N_OUT, tile - 2) <= 0):
                                    pe.wait_ge(out_copied, nth(v, N_OUT, tile - 2))
                            gs = range(4 * second, 4 * second + 4)
                            mm = product([op[tile % 2][:, :]],
                                         [(vh[:, frame % 2, g, span(m, m + 1)], vl[:, frame % 2, g, span(m, m + 1)])
                                          for g in gs],
                                         [[(ph[:, half, g, :], pl[:, half, g, :])] for g in gs],
                                         start=not second, stop=second)
                            if second:
                                mm.then_inc(out_done, 1)

                    def slot(v, k, first=False, last=False):
                        step, strip = divmod(k, STRIPS)
                        scores(v, k, last)
                        if strip == STRIPS - 1 and not (last and step == STEPS - 1):
                            make_z(v, step + 1 if step < STEPS - 1 else STEPS)
                        if not (first and k == 0):
                            turn(v, k - 1)
                        if not (first and k < LAG):
                            attend(v, k)
                        if strip == 4:
                            make_values(v, step + 1)
                        if k == SLOTS - 2 and not last:
                            make_values(v, T)

                    make_values(0, 0)
                    make_z(0, 0)
                    for k in range(HEAD):
                        slot(0, k, first=True)
                    with pe.Fori(0, VIDEOS - 1) as v:
                        for k in range(HEAD, SLOTS):
                            slot(v, k)
                        for k in range(HEAD):
                            slot(v + 1, k)
                    for k in range(HEAD, SLOTS):
                        slot(VIDEOS - 1, k, last=True)
                    turn(VIDEOS, -1)
                    for k in range(LAG):
                        attend(VIDEOS, k)

                @block.scalar
                def _(act):
                    act.wait_ge(prep_mm, 1)
                    nc.scalar.activation(mh[:], sp[0][:, :, 0:C], ACT.Copy, scale=SCALE).then_inc(prep_hi, 1)
                    nc.scalar.activation(wvh[:, :, 0:C], sp[1][:, :, 0:C], ACT.Copy).then_inc(prep_hi, 1)

                    def split_x(v, frame, c):
                        act.wait_ge(x_loaded, 16 * nth(v, T, frame))
                        if frame == T:
                            act.wait_ge(scores_done, nth(v, N_STRIP, SLOTS - 5))
                        elif not (isinstance(v, int) and nth(v, N_STRIP, STRIPS * (frame - 1) - 1) <= 0):
                            act.wait_ge(scores_done, nth(v, N_STRIP, STRIPS * (frame - 1) - 1))
                        nc.scalar.activation(xh[:, frame % T % XRING, c, :], raw[:, c, :], ACT.Copy).then_inc(x_hi, 1)

                    def values_hi_of(v, frame):
                        for j in range(4):
                            act.wait_ge(values_added, nth(v, N_VAL, 4 * frame + j))
                            nc.scalar.activation(vh[:, frame % 2, 2 * j:2 * j + 2, :], vsum[:, j % 2, :, 0:C],
                                                 ACT.Copy).then_inc(values_hi, 1)

                    def z_hi_of(v, index):
                        for m in range(2):
                            act.wait_ge(z_done, nth(v, N_Z, index + m))
                            nc.scalar.activation(zh[:, m, :], sp[BUFFER["z", index + m]][:].rearrange("p a b -> p (a b)"),
                                                 ACT.Identity, bias=u_c[:, m:m + 1]).then_inc(z_hi, 1)

                    def turned_hi_of(v, k):
                        half, strip = (k // 4) % 2, k % 4
                        act.wait_ge(turned, nth(v, N_STRIP, k))
                        nc.scalar.activation(ph[:, half, :, span(strip, strip + 1)], tp[:], ACT.Copy).then_inc(turned_hi, 1)

                    def copy_out(v, k):
                        _, _, _, second = out_quarter(k)
                        if second:
                            for _, tile in out_tiles(k):
                                act.wait_ge(out_done, nth(v, N_OUT, tile))
                                if not (isinstance(v, int) and nth(v, N_OUT, tile - STAGES) <= 0):
                                    act.wait_ge(out_stored[tile % STAGES],
                                                16 * (v * (N_OUT // STAGES) + (tile - tile % STAGES) // STAGES))
                                    act.wait_ge(stats_done, nth(v, N_OUT, tile - STAGES))
                                nc.scalar.activation(stage[:, tile % STAGES, :], op[tile % 2][:], ACT.Copy
                                                     ).then_inc(out_copied, 1)

                    def slot(v, k, first=False, last=False):
                        step, strip = divmod(k, STRIPS)
                        act.wait_ge(shift_done, nth(v, N_STRIP, k))
                        if not (first and k < 2):
                            act.wait_ge(turned, nth(v, N_STRIP, k - 2))
                        nc.scalar.activation(probs[:, k % 2, :], sp[BUFFER["scores", k]][:].rearrange("p a b -> p (a b)"),
                                             ACT.Exp, bias=shift[:, k % 2:k % 2 + 1],
                                             accum_out=total[:, k % 2:k % 2 + 1]).then_inc(exp_done, 1)
                        if strip == STRIPS - 1 and not (last and step == STEPS - 1):
                            z_hi_of(v, 2 * (step + 1))
                        if not (first and k == 0):
                            turned_hi_of(v, k - 1)
                        if not (first and k < LAG):
                            copy_out(v, k)
                        if strip == 4:
                            values_hi_of(v, step + 1)
                        if k == SLOTS - 2 and not last:
                            values_hi_of(v, T)
                        if strip < 2:
                            split_x(v, step + 1, strip)
                        if k in (SLOTS - 4, SLOTS - 3) and not last:
                            split_x(v, T, k - (SLOTS - 4))

                    for c in range(2):
                        act.wait_ge(x_loaded, 16)
                        nc.scalar.activation(xh[:, 0, c, :], raw[:, c, :], ACT.Copy).then_inc(x_hi, 1)
                    values_hi_of(0, 0)
                    z_hi_of(0, 0)
                    for k in range(HEAD):
                        slot(0, k, first=True)
                    with act.Fori(0, VIDEOS - 1) as v:
                        for k in range(HEAD, SLOTS):
                            slot(v, k)
                        for k in range(HEAD):
                            slot(v + 1, k)
                    for k in range(HEAD, SLOTS):
                        slot(VIDEOS - 1, k, last=True)
                    turned_hi_of(VIDEOS, -1)
                    for k in range(LAG):
                        copy_out(VIDEOS, k)

                @block.vector
                def _(dve):
                    nc.vector.memset(wvh[:, :, CW - 1:CW].bitcast(F32), 0.0)
                    nc.vector.memset(wvl[:, :, CW - 1:CW].bitcast(F32), 0.0)
                    dve.wait_ge(weights_loaded, 16 * 9)
                    nc.vector.memset(vbias[:, :, CW - 1:CW], 0.0)
                    dve.wait_ge(prep_mm, 1)
                    nc.vector.tensor_scalar(u_c[:], op[0][:, 0:2], SCALE, None, ALU.mult)
                    for j in range(2):
                        nc.vector.tensor_scalar(vbias[:, j, C:C + 1], op[0][:, 4:5], SCALE, None, ALU.mult)
                        nc.vector.tensor_scalar(wvh[:, j, C:C + 1], op[0][:, 2 + j:3 + j], SCALE, None, ALU.mult
                                                ).then_inc(prep_hi, 1)
                    dve.wait_ge(prep_hi, 4)
                    for j in range(2):
                        nc.vector.scalar_tensor_tensor(out=wvl[:, j, C:C + 1], in0=op[0][:, 2 + j:3 + j], scalar=SCALE,
                                                       in1=wvh[:, j, C:C + 1].bitcast(F32), op0=ALU.mult, op1=ALU.subtract)
                    nc.vector.scalar_tensor_tensor(out=ml[:], in0=sp[0][:, :, 0:C], scalar=SCALE, in1=mh[:].bitcast(F32),
                                                   op0=ALU.mult, op1=ALU.subtract)
                    nc.vector.tensor_tensor(wvl[:, :, 0:C], sp[1][:, :, 0:C], wvh[:, :, 0:C].bitcast(F32),
                                            ALU.subtract).then_inc(prep_ready, 1)

                    def split_x(v, frame, c):
                        q = frame % T % XRING
                        dve.wait_ge(x_hi, nth(v, N_SPLIT, 2 * frame + c))
                        nc.vector.tensor_tensor(xl[:, q, c, :], raw[:, c, :], xh[:, q, c, :].bitcast(F32),
                                                ALU.subtract).then_inc(x_split, 1)

                    def values_of(v, frame):
                        def add(j):
                            index = 4 * frame + j
                            dve.wait_ge(values_done, nth(v, N_VAL, index))
                            if index >= 2:
                                dve.wait_ge(values_split, nth(v, N_VAL, index - 2))
                            nc.vector.tensor_tensor(vsum[:, j % 2, :, :], sp[BUFFER["values", index]][:, :, 0:CW],
                                                    vbias[:], ALU.add).then_inc(values_added, 1)

                        def lo(j):
                            dve.wait_ge(values_hi, nth(v, N_VAL, 4 * frame + j))
                            nc.vector.tensor_copy(r_all[:, frame % T, 2 * j:2 * j + 2], vsum[:, j % 2, :, C])
                            nc.vector.tensor_tensor(vl[:, frame % 2, 2 * j:2 * j + 2, :], vsum[:, j % 2, :, 0:C],
                                                    vh[:, frame % 2, 2 * j:2 * j + 2, :].bitcast(F32),
                                                    ALU.subtract).then_inc(values_split, 1)

                        add(0)
                        for j in range(4):
                            if j < 3:
                                add(j + 1)
                            lo(j)

                    def z_lo_of(v, index):
                        for m in range(2):
                            dve.wait_ge(z_hi, nth(v, N_Z, index + m))
                            nc.vector.scalar_tensor_tensor(
                                out=zl[:, m, :], in0=sp[BUFFER["z", index + m]][:].rearrange("p a b -> p (a b)"),
                                scalar=u_c[:, m:m + 1], in1=zh[:, m, :].bitcast(F32), op0=ALU.add,
                                op1=ALU.subtract).then_inc(z_split, 1)

                    def turned_lo_of(v, k):
                        half, a = (k // 4) % 2, span(k % 4, k % 4 + 1)
                        dve.wait_ge(turned_hi, nth(v, N_STRIP, k))
                        nc.vector.tensor_tensor(pl[:, half, :, a], tp[:], ph[:, half, :, a].bitcast(F32),
                                                ALU.subtract).then_inc(turned_split, 1)

                    def statistics(v, k):
                        _, half, m, second = out_quarter(k)
                        if second:
                            for frame, tile in out_tiles(k):
                                n = (v * T + (frame if tile >= 0 else frame - T)) * 2 + half
                                dve.wait_ge(out_copied, nth(v, N_OUT, tile))
                                nc.vector.bn_stats(stats[:, m, n, :], stage[:, tile % STAGES, :]).then_inc(stats_done, 1)

                    def slot(v, k, first=False, last=False):
                        step, strip = divmod(k, STRIPS)
                        two = slice(k % 2, k % 2 + 1)
                        r = r_all[:, step, strip:strip + 1]
                        dve.wait_ge(scores_done, nth(v, N_STRIP, k))
                        nc.vector.tensor_reduce(negmax[:, two], sp[BUFFER["scores", k]][:].rearrange("p a b -> p (a b)"),
                                                AX_X, ALU.max, negate=True).then_inc(max_done, 1)
                        dve.wait_ge(max_done, nth(v, N_STRIP, k))
                        nc.vector.scalar_tensor_tensor(out=shift[:, two], in0=negmax[:, two], scalar=r, in1=r,
                                                       op0=ALU.subtract, op1=ALU.add).then_inc(shift_done, 1)
                        if strip == STRIPS - 1 and not (last and step == STEPS - 1):
                            z_lo_of(v, 2 * (step + 1))
                        dve.wait_ge(exp_done, nth(v, N_STRIP, k))
                        nc.vector.reciprocal(inverse[:, two], total[:, two]).then_inc(recip_done, 1)
                        dve.wait_ge(recip_done, nth(v, N_STRIP, k))
                        nc.vector.tensor_scalar(probs[:, k % 2, :], probs[:, k % 2, :], inverse[:, two], None,
                                                ALU.mult).then_inc(probs_done, 1)
                        if not (first and k == 0):
                            turned_lo_of(v, k - 1)
                        if not (first and k < LAG):
                            statistics(v, k)
                        if strip == 4:
                            values_of(v, step + 1)
                        if k == SLOTS - 2 and not last:
                            values_of(v, T)
                        if strip < 2:
                            split_x(v, step + 1, strip)
                        if k in (SLOTS - 4, SLOTS - 3) and not last:
                            split_x(v, T, k - (SLOTS - 4))

                    for c in range(2):
                        split_x(0, 0, c)
                    values_of(0, 0)
                    z_lo_of(0, 0)
                    for k in range(HEAD):
                        slot(0, k, first=True)
                    with dve.Fori(0, VIDEOS - 1) as v:
                        for k in range(HEAD, SLOTS):
                            slot(v, k)
                        for k in range(HEAD):
                            slot(v + 1, k)
                    for k in range(HEAD, SLOTS):
                        slot(VIDEOS - 1, k, last=True)
                    turned_lo_of(VIDEOS, -1)
                    for k in range(LAG):
                        statistics(VIDEOS, k)

        RING = 6
        with ExitStack() as two:
            a_ring = sb("a_ring", [P, RING, 2, HW], F32, two)
            x_ring = sb("x_ring", [P, RING, 2, HW], F32, two)
            moments = sb("moments", [P, 2, 2], F32, two)
            root = sb("root", [P, 2], F32, two)
            guess = sb("guess", [P, 2], F32, two)
            error = sb("error", [P, 2], F32, two)
            gain = sb("gain", [P, 2], F32, two)
            offset = sb("offset", [P, 2], F32, two)
            varied = sb("varied", [P, 2], F32, two)
            chain = sem("chain")
            var_ready = sem("var_ready")
            root_ready = sem("root_ready")
            affine_ready = sem("affine_ready")
            pair_loaded = [sem(f"pair_loaded{i}") for i in range(RING)]
            pair_scaled = sem("pair_scaled")
            pair_summed = sem("pair_summed")
            pair_stored = [sem(f"pair_stored{i}") for i in range(RING)]
            ROUNDS = N // RING
            REST = N - ROUNDS * RING

            with nc.Block() as block:

                @block.sync
                def _(sp_):
                    def load(n, i):
                        sp_.dma_start(a_ring[:, i], attended_d[n]).then_inc(pair_loaded[i], 16)
                        sp_.dma_start(x_ring[:, i], x_d[n]).then_inc(pair_loaded[i], 16)

                    for i in range(RING):
                        load(i, i)
                    with sp_.Fori(1, ROUNDS) as g:
                        for i in range(RING):
                            sp_.wait_ge(pair_stored[i], 16 * g)
                            load(g * RING + i, i)
                    for i in range(REST):
                        sp_.wait_ge(pair_stored[i], 16 * ROUNDS)
                        load(ROUNDS * RING + i, i)

                @block.scalar
                def _(act):
                    act.wait_ge(var_ready, 1)
                    nc.scalar.activation(root[:], varied[:], ACT.Sqrt).then_inc(root_ready, 1)
                    act.wait_ge(affine_ready, 1)

                    def scale(n, i, g):
                        act.wait_ge(pair_loaded[i], 32 * (g + 1))
                        for c in range(2):
                            nc.scalar.activation(a_ring[:, i, c, :], a_ring[:, i, c, :], ACT.Identity,
                                                 bias=offset[:, c:c + 1], scale=gain[:, c:c + 1]
                                                 ).then_inc(pair_scaled, 1)

                    def store(n, i):
                        act.wait_ge(pair_summed, 2 * (n + 1))
                        act.dma_start(out_d[n], a_ring[:, i]).then_inc(pair_stored[i], 16)

                    scale(0, 0, 0)
                    for i in range(1, RING):
                        scale(i, i, 0)
                        store(i - 1, i - 1)
                    with act.Fori(1, ROUNDS) as g:
                        for i in range(RING):
                            store(g * RING + i - 1, (i - 1) % RING)
                            scale(g * RING + i, i, g)
                    for i in range(REST):
                        store(ROUNDS * RING + i - 1, (i - 1) % RING)
                        scale(ROUNDS * RING + i, i, ROUNDS)
                    store(N - 1, (N - 1) % RING)
                    for i in range(RING):
                        act.wait_ge(pair_stored[i], 16 * (ROUNDS + (i < REST)))

                @block.vector
                def _(dve):
                    links = [0]

                    def link(ins):
                        links[0] += 1
                        ins.then_inc(chain, 1)
                        dve.wait_ge(chain, links[0])

                    for c in range(2):
                        link(nc.vector.bn_aggr(moments[:, c, :], stats[:, c, :, :].rearrange("p n s -> p (n s)")))
                    link(nc.vector.tensor_scalar(varied[:], moments[:, :, 1], EPS, None, ALU.add))
                    nc.vector.tensor_scalar(error[:], varied[:], 1.0, None, ALU.mult).then_inc(var_ready, 1)
                    dve.wait_ge(root_ready, 1)
                    link(nc.vector.reciprocal(guess[:], root[:]))
                    for _ in range(2):
                        link(nc.vector.tensor_tensor(error[:], guess[:], guess[:], ALU.mult))
                        link(nc.vector.tensor_tensor(error[:], error[:], varied[:], ALU.mult))
                        link(nc.vector.tensor_scalar(error[:], error[:], -0.5, 1.5, ALU.mult, ALU.add))
                        link(nc.vector.tensor_tensor(guess[:], guess[:], error[:], ALU.mult))
                    link(nc.vector.tensor_tensor(gain[:], guess[:], gamma_c[:], ALU.mult))
                    link(nc.vector.tensor_tensor(error[:], gain[:], moments[:, :, 0], ALU.mult))
                    nc.vector.tensor_tensor(offset[:], beta_c[:], error[:], ALU.subtract).then_inc(affine_ready, 1)

                    def add(n, i):
                        for c in range(2):
                            dve.wait_ge(pair_scaled, 2 * n + c + 1)
                            nc.vector.tensor_tensor(a_ring[:, i, c, :], a_ring[:, i, c, :], x_ring[:, i, c, :],
                                                    ALU.add).then_inc(pair_summed, 1)

                    with dve.Fori(0, ROUNDS) as g:
                        for i in range(RING):
                            add(g * RING + i, i)
                    for i in range(REST):
                        add(ROUNDS * RING + i, i)


_INS = ["x", "L0_conv_w1", "L0_conv_b1", "L0_conv_w2", "L0_conv_b2", "L0_conv_w0", "L0_conv_b0", "L0_conv_gamma",
        "L0_conv_beta"]


def kernel(**inputs):
    import numpy as _np
    import concourse.bacc as _bacc
    from concourse import mybir as _mybir
    from concourse.bass_utils import run_bass_kernel_spmd as _run

    nc = _bacc.Bacc("TRN2", target_bir_lowering=False, num_devices=1)
    arrays, args = {}, []
    for name in _INS:
        a = _np.ascontiguousarray(inputs[name])
        arrays[f"in_{name}_dram"] = a
        args.append(nc.dram_tensor(f"in_{name}_dram", a.shape, _mybir.dt.from_np(a.dtype), kind="ExternalInput").ap())
    y = nc.dram_tensor("out_0_dram", inputs["x"].shape, _mybir.dt.float32, kind="ExternalOutput").ap()
    conv_attention_norm(nc, *args, y)
    r = _run(nc, [arrays], core_ids=[0])
    return r.results[0]["out_0_dram"]
```

```python
from contextlib import ExitStack

import numpy as np

import concourse.bass as bass
from concourse import mybir
from concourse.alu_op_type import AluOpType as ALU

ACT = mybir.ActivationFunctionType
F32 = mybir.dt.float32
F32R = mybir.dt.float32r
AX_X = mybir.AxisListType.X

P = 128
T = 8
SBUF_START = 16640
EPS = 1e-5
STEPS = T - 1
STRIPS = 8
SLOTS = STEPS * STRIPS
LAG = 5
HEAD = 9
XRING = 3
STAGES = 4

N_STRIP = SLOTS
N_Z = 2 * STEPS
N_VAL = 4 * T
N_SPLIT = 2 * T
N_OUT = 4 * T


def nth(v, per_video, index):
    return v * per_video + (index + 1)


def units_of_slot(k):
    units = [("scores", k)]
    step, strip = divmod(k, STRIPS)
    if strip == STRIPS - 1:
        units += [("z", 2 * (step + 1) + m) for m in range(2)]
    if strip == 4:
        units += [("values", 4 * (step + 1) + j) for j in range(4)]
    if k == SLOTS - 2:
        units += [("values", N_VAL + j) for j in range(4)]
    return units


UNITS = [u for k in range(SLOTS) for u in units_of_slot(k)]
assert len(UNITS) % 2 == 0
BUFFER = {u: n % 2 for n, u in enumerate(UNITS)}
BUFFER |= {("values", j): BUFFER["values", N_VAL + j] for j in range(4)}
BUFFER |= {("z", m): BUFFER["z", N_Z + m] for m in range(2)}


def before_in_buffer(unit, last):
    n = UNITS.index(unit) - 2
    while last and UNITS[n][0] == "values" and UNITS[n][1] >= N_VAL:
        n -= 2
    kind, index = UNITS[n]
    return (kind, index) if n >= 0 else (kind, index - {"scores": N_STRIP, "z": N_Z, "values": N_VAL}[kind])


def out_quarter(k):
    step, eighth = divmod(k - LAG, STRIPS)
    return step, eighth // 4, eighth % 4 // 2, eighth % 2 == 1


def out_tiles(k):
    step, half, m, _ = out_quarter(k)
    if step == 0:
        return [(f, 4 * half + 2 * m + f) for f in range(2)]
    if step > 0:
        return [(step + 1, 4 * (step + 1) + 2 * half + m)]
    return [(T - 1, 4 * (T - 1) + 2 * half + m - N_OUT)]


def conv_attention_norm(nc, x, w1, b1, w2, b2, w0, b0, gamma, beta, out):
    N, C, H, W = x.shape
    HW = H * W
    VIDEOS = N // T
    assert C == 2 * P and HW == STRIPS * P and N % T == 0
    SCALE = float(C) ** -0.5
    CW = C + 2
    HALF = HW // 2

    x_d = x.rearrange("n (c p) h w -> n p c (h w)", p=P)
    out_d = out.rearrange("n (c p) h w -> n p c (h w)", p=P)
    attended_d = nc.dram_tensor("attended", (N, P, 2, HW), F32, kind="Internal").ap()

    with ExitStack() as ctx:
        def sem(name):
            return ctx.enter_context(nc.semaphore(name))

        places = {}
        top = [SBUF_START]

        def sb(name, shape, dt, at=None):
            size = int(np.prod(shape[1:])) * 4
            places[name] = top[0] if at is None else at
            if at is None:
                top[0] += -(-size // 32) * 32
            return nc.alloc_sbuf_tensor_at(name, shape, dt, offset=places[name])

        def psum(name, shape):
            return ctx.enter_context(nc.psum_tensor(name, shape, F32))

        stats = sb("stats", [P, 2, 2 * N, 6], F32)
        gamma_c = sb("gamma_c", [P, 2], F32)
        beta_c = sb("beta_c", [P, 2], F32)

        weights_loaded = sem("weights_loaded")
        ident_zero = sem("ident_zero")
        ident_ready = sem("ident_ready")
        prep_mm = sem("prep_mm")
        prep_hi = sem("prep_hi")
        prep_ready = sem("prep_ready")
        x_loaded = sem("x_loaded")
        x_hi = sem("x_hi")
        x_split = sem("x_split")
        scores_done = sem("scores_done")
        max_done = sem("max_done")
        shift_done = sem("shift_done")
        exp_done = sem("exp_done")
        recip_done = sem("recip_done")
        probs_done = sem("probs_done")
        turned = sem("turned")
        turned_hi = sem("turned_hi")
        turned_split = sem("turned_split")
        z_done = sem("z_done")
        z_hi = sem("z_hi")
        z_split = sem("z_split")
        values_done = sem("values_done")
        values_added = sem("values_added")
        values_hi = sem("values_hi")
        values_split = sem("values_split")
        out_done = sem("out_done")
        out_copied = sem("out_copied")
        stats_done = sem("stats_done")
        out_stored = [sem(f"out_stored{i}") for i in range(STAGES)]

        xs = sb("xs", [P, XRING, 2, 2, HW], F32R)
        zs = sb("zs", [P, 2, 2, HW], F32R)
        vs = sb("vs", [P, 2, 2, STRIPS, C], F32R)
        ps = sb("ps", [P, 2, 2, STRIPS, HALF], F32R)
        probs = sb("probs", [P, 2, HW], F32)
        raw = sb("raw", [P, 2, HW], F32)
        vsum = sb("vsum", [P, 2, 2, CW], F32)
        stage = sb("stage", [P, STAGES, HALF], F32)
        mh = sb("mh", [P, 2, C], F32R)
        ml = sb("ml", [P, 2, C], F32R)
        wvh = sb("wvh", [P, 2, CW], F32R)
        wvl = sb("wvl", [P, 2, CW], F32R)
        vbias = sb("vbias", [P, 2, CW], F32)
        u_c = sb("u_c", [P, 2], F32)
        b1_c = sb("b1_c", [P, 2], F32)
        b2_c = sb("b2_c", [P, 2], F32)
        ident = sb("ident", [P, P], F32)
        r_all = sb("r_all", [P, T, STRIPS], F32)
        negmax = sb("negmax", [P, 2], F32)
        shift = sb("shift", [P, 2], F32)
        total = sb("total", [P, 2], F32)
        inverse = sb("inverse", [P, 2], F32)
        xh, xl = xs[:, :, 0], xs[:, :, 1]
        zh, zl = zs[:, 0], zs[:, 1]
        vh, vl = vs[:, :, 0], vs[:, :, 1]
        ph, pl = ps[:, :, 0], ps[:, :, 1]

        sp = [psum(f"sp{i}", [P, 2, HALF]) for i in range(2)]
        tp = psum("tp", [P, STRIPS, P])
        op = [psum(f"op{i}", [P, HALF]) for i in range(2)]

        FRAME = 2 * HW * 4
        homes = [("xs", 0), ("vs", 0), ("xs", 2), ("xs", 4), ("zs", 0), ("ps", 0), ("ps", 2), ("probs", 0)]
        RING = len(homes)
        ROUNDS = N // RING
        assert N % RING == 0
        pairs = [sb(f"pair{i}", [P, 2, 2, HW], F32, at=places[name] + k * FRAME) for i, (name, k) in enumerate(homes)]
        moments = sb("moments", [P, 2, 2], F32)
        varied = sb("varied", [P, 2], F32)
        root = sb("root", [P, 2], F32)
        guess = sb("guess", [P, 2], F32)
        error = sb("error", [P, 2], F32)
        gain = sb("gain", [P, 2], F32)
        offset = sb("offset", [P, 2], F32)
        chain = sem("chain")
        var_ready = sem("var_ready")
        root_ready = sem("root_ready")
        affine_ready = sem("affine_ready")
        pair_loaded = [sem(f"pair_loaded{i}") for i in range(RING)]
        pair_scaled = sem("pair_scaled")
        pair_summed = sem("pair_summed")
        pair_stored = [sem(f"pair_stored{i}") for i in range(RING)]

        w1_s = probs[:, 0, 0:2 * C].rearrange("p (t c) -> p t c", t=2)
        w2_s = probs[:, 0, 2 * C:4 * C].rearrange("p (t c) -> p t c", t=2)
        w0_s = probs[:, 1, 0:2 * C].rearrange("p (t c) -> p t c", t=2)

        def span(a, b):
            return slice(a * P, b * P)

        with nc.Block() as block:

            @block.gpsimd
            def _(pool):
                nc.gpsimd.memset(ident[:], 0.0).then_inc(ident_zero, 1)
                pool.wait_ge(ident_zero, 1)
                nc.gpsimd.affine_select(out=ident[:], in_=ident[:], compare_op=ALU.not_equal, fill=1.0,
                                        base=0, pattern=[[-1, P]], channel_multiplier=1).then_inc(ident_ready, 1)

            @block.sync
            def _(sp_):
                for dst, src in ((w1_s, w1), (w2_s, w2), (w0_s, w0)):
                    sp_.dma_start(dst, src.rearrange("(t p) c -> p t c", p=P)).then_inc(weights_loaded, 16)
                with nc.allow_non_contiguous_dma(reason="five columns of 256 numbers"):
                    for dst, src in ((b1_c, b1), (b2_c, b2), (gamma_c, gamma), (beta_c, beta)):
                        sp_.dma_start(dst[:], src.rearrange("(t p) -> p t", p=P)).then_inc(weights_loaded, 16)
                for j in range(2):
                    sp_.dma_start(vbias[:, j, 0:C], b0.partition_broadcast(P)).then_inc(weights_loaded, 16)
                sp_.dma_start(raw[:], x_d[0]).then_inc(x_loaded, 16)
                sp_.wait_ge(x_split, 2)
                sp_.dma_start(raw[:], x_d[1]).then_inc(x_loaded, 16)

                def load_pair(n, i):
                    sp_.dma_start(pairs[i][:, 0], attended_d[n]).then_inc(pair_loaded[i], 16)
                    sp_.dma_start(pairs[i][:, 1], x_d[n]).then_inc(pair_loaded[i], 16)

                def slot(v, k, first=False, last=False, tail=False):
                    step, strip = divmod(k, STRIPS)
                    load = step + 2 if strip == 2 else T + 1 if k == SLOTS - 2 else None
                    if load is not None and not tail and not (last and load >= T):
                        sp_.wait_ge(x_split, nth(v, N_SPLIT, 2 * load - 1))
                        sp_.dma_start(raw[:], x_d[v * T + load]).then_inc(x_loaded, 16)
                    _, half, m, second = out_quarter(k)
                    if second and not (first and k < LAG):
                        for frame, tile in out_tiles(k):
                            n = v * T + (frame if tile >= 0 else frame - T)
                            sp_.wait_ge(out_copied, nth(v, N_OUT, tile))
                            sp_.dma_start(attended_d[n][:, m, half * HALF:(half + 1) * HALF],
                                          stage[:, tile % STAGES, :]).then_inc(out_stored[tile % STAGES], 16)

                for k in range(HEAD):
                    slot(0, k, first=True)
                with sp_.Fori(0, VIDEOS - 1) as v:
                    for k in range(HEAD, SLOTS):
                        slot(v, k)
                    for k in range(HEAD):
                        slot(v + 1, k)
                end = VIDEOS - 1
                left = {
                    STRIPS * 6: [(0, z_done, nth(end, N_Z, 2 * 6 + 1))],
                    STRIPS * 6 + LAG: [(1, out_done, nth(end, N_OUT, 4 * 6 + 3)),
                                       (2, values_done, nth(end, N_VAL, 4 * 7 + 3))],
                    SLOTS: [(3, scores_done, VIDEOS * N_STRIP), (4, scores_done, VIDEOS * N_STRIP)],
                    SLOTS + 1: [(5, out_done, nth(end, N_OUT, 4 * 7 + 1)), (6, out_done, nth(end, N_OUT, 4 * 7 + 1)),
                                (7, turned, VIDEOS * N_STRIP)],
                }
                for k in range(HEAD, SLOTS + LAG):
                    if k < SLOTS:
                        slot(end, k, last=True)
                    else:
                        slot(VIDEOS, k - SLOTS, tail=True)
                    if k == STRIPS * 6:
                        for s in out_stored:
                            sp_.wait_ge(s, 16 * end * N_OUT // STAGES)
                    for i, done, count in left.get(k, []):
                        sp_.wait_ge(done, count)
                        load_pair(i, i)
                for s in out_stored:
                    sp_.wait_ge(s, 16 * VIDEOS * N_OUT // STAGES)
                with sp_.Fori(1, ROUNDS) as g:
                    for i in range(RING):
                        sp_.wait_ge(pair_stored[i], 16 * g)
                        load_pair(g * RING + i, i)

            @block.tensor
            def _(pe):
                def product(outs, weights, movings, start=True, stop=True):
                    n = len(weights)
                    for c, (w_hi, w_lo) in enumerate(weights):
                        for w, part in ((w_hi, 0), (w_hi, 1), (w_lo, 0)):
                            for h, o in enumerate(outs):
                                mm = nc.tensor.matmul(o, w, movings[c][h][part],
                                                      start=start and c == 0 and part == 0 and w is w_hi,
                                                      stop=stop and c == n - 1 and w is w_lo)
                    return mm

                pe.wait_ge(weights_loaded, 16 * 9)
                pe.wait_ge(ident_ready, 1)
                for i in range(2):
                    for o in range(2):
                        nc.tensor.matmul(sp[0][:, i, 0:C], w1_s[:, o, span(i, i + 1)], w2_s[:, o, :],
                                         start=o == 0, stop=o == 1)
                for i in range(2):
                    for o in range(2):
                        nc.tensor.transpose(sp[1][:, i, span(o, o + 1)], w0_s[:, o, span(i, i + 1)], ident[:])
                for at, (w, b) in enumerate(((w2_s, b1_c), (w1_s, b2_c))):
                    for m in range(2):
                        for o in range(2):
                            nc.tensor.matmul(op[0][:, 2 * at + m:2 * at + m + 1], w[:, o, span(m, m + 1)],
                                             b[:, o:o + 1], start=o == 0, stop=o == 1)
                for o in range(2):
                    mm = nc.tensor.matmul(op[0][:, 4:5], b1_c[:, o:o + 1].to_broadcast([P, P]),
                                          b2_c[:, o:o + 1], start=o == 0, stop=o == 1)
                mm.then_inc(prep_mm, 1)

                def wait_buffer(v, unit, last=False):
                    kind, index = before_in_buffer(unit, last)
                    if kind == "scores":
                        if not (isinstance(v, int) and nth(v, N_STRIP, index) <= 0):
                            pe.wait_ge(exp_done, nth(v, N_STRIP, index))
                    elif kind == "z":
                        pe.wait_ge(z_split, nth(v, N_Z, index))
                    else:
                        pe.wait_ge(values_added, nth(v, N_VAL, index))

                def scores(v, k, last):
                    step, strip = divmod(k, STRIPS)
                    key = max(step - 1, 0) % XRING
                    if isinstance(v, int) and v == 0 and k < 2:
                        pe.wait_ge(values_added, 4)
                    else:
                        wait_buffer(v, ("scores", k), last)
                    if strip == 0:
                        pe.wait_ge(z_split, nth(v, N_Z, 2 * step + 1))
                    a = span(strip, strip + 1)
                    halves = [slice(h * HALF, (h + 1) * HALF) for h in range(2)]
                    product([sp[BUFFER["scores", k]][:, h, :] for h in range(2)],
                            [(zh[:, c, a], zl[:, c, a]) for c in range(2)],
                            [[(xh[:, key, c, s], xl[:, key, c, s]) for s in halves] for c in range(2)]
                            ).then_inc(scores_done, 1)

                def make_z(v, frame):
                    for m in range(2):
                        index = 2 * frame + m
                        q = frame % STEPS % XRING
                        if index >= 2:
                            wait_buffer(v, ("z", index))
                        else:
                            pe.wait_ge(prep_ready, 1)
                        pe.wait_ge(x_split, nth(v, N_SPLIT, 2 * (frame if frame < STEPS else T) + 1))
                        halves = [slice(h * HALF, (h + 1) * HALF) for h in range(2)]
                        product([sp[BUFFER["z", index]][:, h, :] for h in range(2)],
                                [(mh[:, c, span(m, m + 1)], ml[:, c, span(m, m + 1)]) for c in range(2)],
                                [[(xh[:, q, c, s], xl[:, q, c, s]) for s in halves] for c in range(2)]
                                ).then_inc(z_done, 1)

                def make_values(v, frame):
                    q = frame % T % XRING
                    for j in range(4):
                        index = 4 * frame + j
                        if index >= 4:
                            wait_buffer(v, ("values", index))
                        elif j >= 2:
                            pe.wait_ge(values_added, j - 1)
                        else:
                            pe.wait_ge(z_split, 2)
                        pe.wait_ge(x_split, nth(v, N_SPLIT, 2 * frame + 1))
                        for i in range(2):
                            a = span(2 * j + i, 2 * j + i + 1)
                            mm = product([sp[BUFFER["values", index]][:, i, 0:CW]],
                                         [(xh[:, q, c, a], xl[:, q, c, a]) for c in range(2)],
                                         [[(wvh[:, c, :], wvl[:, c, :])] for c in range(2)])
                        mm.then_inc(values_done, 1)

                def turn(v, k):
                    pe.wait_ge(probs_done, nth(v, N_STRIP, k))
                    if not (isinstance(v, int) and nth(v, N_STRIP, k - 1) <= 0):
                        pe.wait_ge(turned_split, nth(v, N_STRIP, k - 1))
                    for j in range(STRIPS):
                        tr = nc.tensor.transpose(tp[:, j, :], probs[:, k % 2, span(j, j + 1)], ident[:])
                    tr.then_inc(turned, 1)

                def attend(v, k):
                    step, half, m, second = out_quarter(k)
                    for frame, tile in out_tiles(k):
                        if not second:
                            if m == 0:
                                pe.wait_ge(turned_split, nth(v, N_STRIP, STRIPS * step + 4 * half + 3))
                                pe.wait_ge(values_split, nth(v, N_VAL, 4 * (step + 1) + 3 if step >= 0 else -1))
                            if not (isinstance(v, int) and nth(v, N_OUT, tile - 2) <= 0):
                                pe.wait_ge(out_copied, nth(v, N_OUT, tile - 2))
                        gs = range(4 * second, 4 * second + 4)
                        mm = product([op[tile % 2][:, :]],
                                     [(vh[:, frame % 2, g, span(m, m + 1)], vl[:, frame % 2, g, span(m, m + 1)])
                                      for g in gs],
                                     [[(ph[:, half, g, :], pl[:, half, g, :])] for g in gs],
                                     start=not second, stop=second)
                        if second:
                            mm.then_inc(out_done, 1)

                def slot(v, k, first=False, last=False):
                    step, strip = divmod(k, STRIPS)
                    scores(v, k, last)
                    if strip == STRIPS - 1 and not (last and step == STEPS - 1):
                        make_z(v, step + 1 if step < STEPS - 1 else STEPS)
                    if not (first and k == 0):
                        turn(v, k - 1)
                    if not (first and k < LAG):
                        attend(v, k)
                    if strip == 4:
                        make_values(v, step + 1)
                    if k == SLOTS - 2 and not last:
                        make_values(v, T)

                make_z(0, 0)
                make_values(0, 0)
                for k in range(HEAD):
                    slot(0, k, first=True)
                with pe.Fori(0, VIDEOS - 1) as v:
                    for k in range(HEAD, SLOTS):
                        slot(v, k)
                    for k in range(HEAD):
                        slot(v + 1, k)
                for k in range(HEAD, SLOTS):
                    slot(VIDEOS - 1, k, last=True)
                turn(VIDEOS, -1)
                for k in range(LAG):
                    attend(VIDEOS, k)

            @block.scalar
            def _(act):
                act.wait_ge(prep_mm, 1)
                nc.scalar.activation(mh[:], sp[0][:, :, 0:C], ACT.Copy, scale=SCALE).then_inc(prep_hi, 1)
                nc.scalar.activation(wvh[:, :, 0:C], sp[1][:, :, 0:C], ACT.Copy).then_inc(prep_hi, 1)

                def split_x(v, frame, c):
                    act.wait_ge(x_loaded, 16 * nth(v, T, frame))
                    if frame == T:
                        act.wait_ge(scores_done, nth(v, N_STRIP, SLOTS - 5))
                    elif not (isinstance(v, int) and nth(v, N_STRIP, STRIPS * (frame - 1) - 1) <= 0):
                        act.wait_ge(scores_done, nth(v, N_STRIP, STRIPS * (frame - 1) - 1))
                    nc.scalar.activation(xh[:, frame % T % XRING, c, :], raw[:, c, :], ACT.Copy).then_inc(x_hi, 1)

                def values_hi_of(v, frame):
                    for j in range(4):
                        act.wait_ge(values_added, nth(v, N_VAL, 4 * frame + j))
                        nc.scalar.activation(vh[:, frame % 2, 2 * j:2 * j + 2, :], vsum[:, j % 2, :, 0:C],
                                             ACT.Copy).then_inc(values_hi, 1)

                def z_hi_of(v, index):
                    for m in range(2):
                        act.wait_ge(z_done, nth(v, N_Z, index + m))
                        nc.scalar.activation(zh[:, m, :], sp[BUFFER["z", index + m]][:].rearrange("p a b -> p (a b)"),
                                             ACT.Identity, bias=u_c[:, m:m + 1]).then_inc(z_hi, 1)

                def turned_hi_of(v, k):
                    half, strip = (k // 4) % 2, k % 4
                    act.wait_ge(turned, nth(v, N_STRIP, k))
                    nc.scalar.activation(ph[:, half, :, span(strip, strip + 1)], tp[:], ACT.Copy).then_inc(turned_hi, 1)

                def copy_out(v, k):
                    _, _, _, second = out_quarter(k)
                    if second:
                        for _, tile in out_tiles(k):
                            act.wait_ge(out_done, nth(v, N_OUT, tile))
                            if not (isinstance(v, int) and nth(v, N_OUT, tile - STAGES) <= 0):
                                act.wait_ge(out_stored[tile % STAGES],
                                            16 * (v * (N_OUT // STAGES) + (tile - tile % STAGES) // STAGES))
                                act.wait_ge(stats_done, nth(v, N_OUT, tile - STAGES))
                            nc.scalar.activation(stage[:, tile % STAGES, :], op[tile % 2][:], ACT.Copy
                                                 ).then_inc(out_copied, 1)

                def slot(v, k, first=False, last=False):
                    step, strip = divmod(k, STRIPS)
                    act.wait_ge(shift_done, nth(v, N_STRIP, k))
                    if not (first and k < 2):
                        act.wait_ge(turned, nth(v, N_STRIP, k - 2))
                    nc.scalar.activation(probs[:, k % 2, :], sp[BUFFER["scores", k]][:].rearrange("p a b -> p (a b)"),
                                         ACT.Exp, bias=shift[:, k % 2:k % 2 + 1],
                                         accum_out=total[:, k % 2:k % 2 + 1]).then_inc(exp_done, 1)
                    if strip == STRIPS - 1 and not (last and step == STEPS - 1):
                        z_hi_of(v, 2 * (step + 1))
                    if not (first and k == 0):
                        turned_hi_of(v, k - 1)
                    if not (first and k < LAG):
                        copy_out(v, k)
                    if strip == 4:
                        values_hi_of(v, step + 1)
                    if k == SLOTS - 2 and not last:
                        values_hi_of(v, T)
                    if strip < 2:
                        split_x(v, step + 1, strip)
                    if k in (SLOTS - 4, SLOTS - 3) and not last:
                        split_x(v, T, k - (SLOTS - 4))

                for c in range(2):
                    act.wait_ge(x_loaded, 16)
                    nc.scalar.activation(xh[:, 0, c, :], raw[:, c, :], ACT.Copy).then_inc(x_hi, 1)
                z_hi_of(0, 0)
                values_hi_of(0, 0)
                for k in range(HEAD):
                    slot(0, k, first=True)
                with act.Fori(0, VIDEOS - 1) as v:
                    for k in range(HEAD, SLOTS):
                        slot(v, k)
                    for k in range(HEAD):
                        slot(v + 1, k)
                for k in range(HEAD, SLOTS):
                    slot(VIDEOS - 1, k, last=True)
                turned_hi_of(VIDEOS, -1)
                for k in range(LAG):
                    copy_out(VIDEOS, k)

                act.wait_ge(var_ready, 1)
                nc.scalar.activation(root[:], varied[:], ACT.Sqrt).then_inc(root_ready, 1)
                act.wait_ge(affine_ready, 1)

                def scale(n, i, g):
                    act.wait_ge(pair_loaded[i], 32 * (g + 1))
                    for c in range(2):
                        nc.scalar.activation(pairs[i][:, 0, c, :], pairs[i][:, 0, c, :], ACT.Identity,
                                             bias=offset[:, c:c + 1], scale=gain[:, c:c + 1]).then_inc(pair_scaled, 1)

                def store(n, i):
                    act.wait_ge(pair_summed, 2 * (n + 1))
                    act.dma_start(out_d[n], pairs[i][:, 0]).then_inc(pair_stored[i], 16)

                scale(0, 0, 0)
                for i in range(1, RING):
                    scale(i, i, 0)
                    store(i - 1, i - 1)
                with act.Fori(1, ROUNDS) as g:
                    for i in range(RING):
                        store(g * RING + i - 1, (i - 1) % RING)
                        scale(g * RING + i, i, g)
                store(N - 1, RING - 1)
                for i in range(RING):
                    act.wait_ge(pair_stored[i], 16 * ROUNDS)

            @block.vector
            def _(dve):
                nc.vector.memset(wvh[:, :, CW - 1:CW].bitcast(F32), 0.0)
                nc.vector.memset(wvl[:, :, CW - 1:CW].bitcast(F32), 0.0)
                dve.wait_ge(weights_loaded, 16 * 9)
                nc.vector.memset(vbias[:, :, CW - 1:CW], 0.0)
                dve.wait_ge(prep_mm, 1)
                nc.vector.tensor_scalar(u_c[:], op[0][:, 0:2], SCALE, None, ALU.mult)
                for j in range(2):
                    nc.vector.tensor_scalar(vbias[:, j, C:C + 1], op[0][:, 4:5], SCALE, None, ALU.mult)
                    nc.vector.tensor_scalar(wvh[:, j, C:C + 1], op[0][:, 2 + j:3 + j], SCALE, None, ALU.mult
                                            ).then_inc(prep_hi, 1)
                dve.wait_ge(prep_hi, 4)
                for j in range(2):
                    nc.vector.scalar_tensor_tensor(out=wvl[:, j, C:C + 1], in0=op[0][:, 2 + j:3 + j], scalar=SCALE,
                                                   in1=wvh[:, j, C:C + 1].bitcast(F32), op0=ALU.mult, op1=ALU.subtract)
                nc.vector.scalar_tensor_tensor(out=ml[:], in0=sp[0][:, :, 0:C], scalar=SCALE, in1=mh[:].bitcast(F32),
                                               op0=ALU.mult, op1=ALU.subtract)
                nc.vector.tensor_tensor(wvl[:, :, 0:C], sp[1][:, :, 0:C], wvh[:, :, 0:C].bitcast(F32),
                                        ALU.subtract).then_inc(prep_ready, 1)

                def split_x(v, frame, c):
                    q = frame % T % XRING
                    dve.wait_ge(x_hi, nth(v, N_SPLIT, 2 * frame + c))
                    nc.vector.tensor_tensor(xl[:, q, c, :], raw[:, c, :], xh[:, q, c, :].bitcast(F32),
                                            ALU.subtract).then_inc(x_split, 1)

                def values_of(v, frame):
                    def add(j):
                        index = 4 * frame + j
                        dve.wait_ge(values_done, nth(v, N_VAL, index))
                        if index >= 2:
                            dve.wait_ge(values_split, nth(v, N_VAL, index - 2))
                        nc.vector.tensor_tensor(vsum[:, j % 2, :, :], sp[BUFFER["values", index]][:, :, 0:CW],
                                                vbias[:], ALU.add).then_inc(values_added, 1)

                    def lo(j):
                        dve.wait_ge(values_hi, nth(v, N_VAL, 4 * frame + j))
                        nc.vector.tensor_copy(r_all[:, frame % T, 2 * j:2 * j + 2], vsum[:, j % 2, :, C])
                        nc.vector.tensor_tensor(vl[:, frame % 2, 2 * j:2 * j + 2, :], vsum[:, j % 2, :, 0:C],
                                                vh[:, frame % 2, 2 * j:2 * j + 2, :].bitcast(F32),
                                                ALU.subtract).then_inc(values_split, 1)

                    add(0)
                    for j in range(4):
                        if j < 3:
                            add(j + 1)
                        lo(j)

                def z_lo_of(v, index):
                    for m in range(2):
                        dve.wait_ge(z_hi, nth(v, N_Z, index + m))
                        nc.vector.scalar_tensor_tensor(
                            out=zl[:, m, :], in0=sp[BUFFER["z", index + m]][:].rearrange("p a b -> p (a b)"),
                            scalar=u_c[:, m:m + 1], in1=zh[:, m, :].bitcast(F32), op0=ALU.add,
                            op1=ALU.subtract).then_inc(z_split, 1)

                def turned_lo_of(v, k):
                    half, a = (k // 4) % 2, span(k % 4, k % 4 + 1)
                    dve.wait_ge(turned_hi, nth(v, N_STRIP, k))
                    nc.vector.tensor_tensor(pl[:, half, :, a], tp[:], ph[:, half, :, a].bitcast(F32),
                                            ALU.subtract).then_inc(turned_split, 1)

                def statistics(v, k):
                    _, half, m, second = out_quarter(k)
                    if second:
                        for frame, tile in out_tiles(k):
                            n = (v * T + (frame if tile >= 0 else frame - T)) * 2 + half
                            dve.wait_ge(out_copied, nth(v, N_OUT, tile))
                            nc.vector.bn_stats(stats[:, m, n, :], stage[:, tile % STAGES, :]).then_inc(stats_done, 1)

                def slot(v, k, first=False, last=False):
                    step, strip = divmod(k, STRIPS)
                    two = slice(k % 2, k % 2 + 1)
                    r = r_all[:, step, strip:strip + 1]
                    dve.wait_ge(scores_done, nth(v, N_STRIP, k))
                    nc.vector.tensor_reduce(negmax[:, two], sp[BUFFER["scores", k]][:].rearrange("p a b -> p (a b)"),
                                            AX_X, ALU.max, negate=True).then_inc(max_done, 1)
                    dve.wait_ge(max_done, nth(v, N_STRIP, k))
                    nc.vector.scalar_tensor_tensor(out=shift[:, two], in0=negmax[:, two], scalar=r, in1=r,
                                                   op0=ALU.subtract, op1=ALU.add).then_inc(shift_done, 1)
                    if strip == STRIPS - 1 and not (last and step == STEPS - 1):
                        z_lo_of(v, 2 * (step + 1))
                    dve.wait_ge(exp_done, nth(v, N_STRIP, k))
                    nc.vector.reciprocal(inverse[:, two], total[:, two]).then_inc(recip_done, 1)
                    dve.wait_ge(recip_done, nth(v, N_STRIP, k))
                    nc.vector.tensor_scalar(probs[:, k % 2, :], probs[:, k % 2, :], inverse[:, two], None,
                                            ALU.mult).then_inc(probs_done, 1)
                    if not (first and k == 0):
                        turned_lo_of(v, k - 1)
                    if not (first and k < LAG):
                        statistics(v, k)
                    if strip == 4:
                        values_of(v, step + 1)
                    if k == SLOTS - 2 and not last:
                        values_of(v, T)
                    if strip < 2:
                        split_x(v, step + 1, strip)
                    if k in (SLOTS - 4, SLOTS - 3) and not last:
                        split_x(v, T, k - (SLOTS - 4))

                for c in range(2):
                    split_x(0, 0, c)
                z_lo_of(0, 0)
                values_of(0, 0)
                for k in range(HEAD):
                    slot(0, k, first=True)
                with dve.Fori(0, VIDEOS - 1) as v:
                    for k in range(HEAD, SLOTS):
                        slot(v, k)
                    for k in range(HEAD):
                        slot(v + 1, k)
                for k in range(HEAD, SLOTS):
                    slot(VIDEOS - 1, k, last=True)
                turned_lo_of(VIDEOS, -1)
                for k in range(LAG):
                    statistics(VIDEOS, k)

                links = [0]

                def link(ins):
                    links[0] += 1
                    ins.then_inc(chain, 1)
                    dve.wait_ge(chain, links[0])

                dve.wait_ge(stats_done, VIDEOS * N_OUT)
                for c in range(2):
                    link(nc.vector.bn_aggr(moments[:, c, :], stats[:, c, :, :].rearrange("p n s -> p (n s)")))
                nc.vector.tensor_scalar(varied[:], moments[:, :, 1], EPS, None, ALU.add).then_inc(var_ready, 1)
                dve.wait_ge(root_ready, 1)
                link(nc.vector.reciprocal(guess[:], root[:]))
                for _ in range(2):
                    link(nc.vector.tensor_tensor(error[:], guess[:], guess[:], ALU.mult))
                    link(nc.vector.tensor_tensor(error[:], error[:], varied[:], ALU.mult))
                    link(nc.vector.tensor_scalar(error[:], error[:], -0.5, 1.5, ALU.mult, ALU.add))
                    link(nc.vector.tensor_tensor(guess[:], guess[:], error[:], ALU.mult))
                link(nc.vector.tensor_tensor(gain[:], guess[:], gamma_c[:], ALU.mult))
                link(nc.vector.tensor_tensor(error[:], gain[:], moments[:, :, 0], ALU.mult))
                nc.vector.tensor_tensor(offset[:], beta_c[:], error[:], ALU.subtract).then_inc(affine_ready, 1)

                with dve.Fori(0, ROUNDS) as g:
                    for i in range(RING):
                        for c in range(2):
                            dve.wait_ge(pair_scaled, 2 * (g * RING + i) + c + 1)
                            nc.vector.tensor_tensor(pairs[i][:, 0, c, :], pairs[i][:, 0, c, :], pairs[i][:, 1, c, :],
                                                    ALU.add).then_inc(pair_summed, 1)

_INS = ["x", "L0_conv_w1", "L0_conv_b1", "L0_conv_w2", "L0_conv_b2", "L0_conv_w0", "L0_conv_b0", "L0_conv_gamma",
        "L0_conv_beta"]


def kernel(**inputs):
    import numpy as _np
    import concourse.bacc as _bacc
    from concourse import mybir as _mybir
    from concourse.bass_utils import run_bass_kernel_spmd as _run

    nc = _bacc.Bacc("TRN2", target_bir_lowering=False, num_devices=1)
    arrays, args = {}, []
    for name in _INS:
        a = _np.ascontiguousarray(inputs[name])
        arrays[f"in_{name}_dram"] = a
        args.append(nc.dram_tensor(f"in_{name}_dram", a.shape, _mybir.dt.from_np(a.dtype), kind="ExternalInput").ap())
    y = nc.dram_tensor("out_0_dram", inputs["x"].shape, _mybir.dt.float32, kind="ExternalOutput").ap()
    conv_attention_norm(nc, *args, y)
    r = _run(nc, [arrays], core_ids=[0])
    return r.results[0]["out_0_dram"]
```

```python
from contextlib import ExitStack

import numpy as np

import concourse.bass as bass
from concourse import mybir
from concourse.alu_op_type import AluOpType as ALU

ACT = mybir.ActivationFunctionType
F32 = mybir.dt.float32
F32R = mybir.dt.float32r
AX_X = mybir.AxisListType.X

P = 128
T = 8
SBUF_START = 16640
EPS = 1e-5
STEPS = T - 1
STRIPS = 8
SLOTS = STEPS * STRIPS
BLOCK = 32
CARRY = 4
LAG = 8
HEAD = 12
XRING = 3
STAGES = 2

N_STRIP = SLOTS
N_PAIR = SLOTS // 4
N_Z = 2 * STEPS
N_VAL = 4 * T
N_SPLIT = 2 * T
N_OUT = 4 * T
CARRIED = 16 * 16


def nth(v, per_video, index):
    return v * per_video + (index + 1)


def values_of_slot(k, last=False):
    step, strip = divmod(k, STRIPS)
    if k == SLOTS - 1:
        return [] if last else [4 * T + j for j in range(4)]
    if step < 2:
        return [4 * (step + 1) + j for j in range(4)] if strip == STRIPS - 1 else []
    return [4 * (step + 1) + 2 * (strip - 4) + j for j in range(2)] if strip in (4, 5) else []


def nth_by_two(v, per_video, index):
    assert per_video % 2 == 0 and index % 2 == 1
    return (v * (per_video // 2) + (index + 1) // 2) * 2


def units_of_slot(k):
    units = [("scores", k)]
    step, strip = divmod(k, STRIPS)
    if strip == STRIPS - 1:
        units += [("z", 2 * (step + 1) + m) for m in range(2)]
    units += [("values", index) for index in values_of_slot(k)]
    return units


BUFFERS = 3
UNITS = [u for k in range(SLOTS) for u in units_of_slot(k)]
assert len(UNITS) % BUFFERS == 0
BUFFER = {u: n % BUFFERS for n, u in enumerate(UNITS)}


def before_in_buffer(unit):
    n = UNITS.index(unit) - BUFFERS
    kind, index = UNITS[n]
    return (kind, index) if n >= 0 else (kind, index - {"scores": N_STRIP, "z": N_Z, "values": N_VAL}[kind])


def out_quarter(k):
    step, eighth = divmod(k - LAG, STRIPS)
    return step, eighth // 4, eighth % 4 // 2, eighth % 2 == 1


def out_tiles(k):
    step, half, m, _ = out_quarter(k)
    if step == 0:
        return [(f, 4 * half + 2 * m + f) for f in range(2)]
    if step > 0:
        return [(step + 1, 4 * (step + 1) + 2 * half + m)]
    frame = step + 1 + STEPS
    return [(frame, 4 * frame + 2 * half + m - N_OUT)]


def conv_attention_norm(nc, x, w1, b1, w2, b2, w0, b0, gamma, beta, out):
    N, C, H, W = x.shape
    HW = H * W
    VIDEOS = N // T
    assert C == 2 * P and HW == STRIPS * P and N % T == 0
    SCALE = float(C) ** -0.5
    CW = C + 2
    HALF = HW // 2

    x_d = x.rearrange("n (c p) h w -> n p c (h w)", p=P)
    out_d = out.rearrange("n (c p) h w -> n p c (h w)", p=P)
    attended_d = nc.dram_tensor("attended", (N, P, 2, HW), F32, kind="Internal").ap()

    with ExitStack() as ctx:
        def sem(name):
            return ctx.enter_context(nc.semaphore(name))

        places = {}
        top = [SBUF_START]

        def sb(name, shape, dt, at=None):
            size = int(np.prod(shape[1:])) * 4
            places[name] = top[0] if at is None else at
            if at is None:
                top[0] += -(-size // 32) * 32
            return nc.alloc_sbuf_tensor_at(name, shape, dt, offset=places[name])

        def psum(name, shape):
            return ctx.enter_context(nc.psum_tensor(name, shape, F32))

        stats = sb("stats", [P, 2, 2 * N, 6], F32)
        gamma_c = sb("gamma_c", [P, 2], F32)
        beta_c = sb("beta_c", [P, 2], F32)

        products_loaded = sem("products_loaded")
        weights_loaded = sem("weights_loaded")
        ident_zero = sem("ident_zero")
        ident_ready = sem("ident_ready")
        columns_loaded = sem("columns_loaded")
        prep_mm = sem("prep_mm")
        prep_hi = sem("prep_hi")
        prep_ready = sem("prep_ready")
        x_loaded = sem("x_loaded")
        x_hi = sem("x_hi")
        x_split = sem("x_split")
        scores_done = sem("scores_done")
        max_done = sem("max_done")
        shift_done = sem("shift_done")
        exp_done = sem("exp_done")
        recip_done = sem("recip_done")
        probs_done = sem("probs_done")
        flipped = sem("flipped")
        carried = [sem(f"carried{i}") for i in range(2)]
        turned_hi = sem("turned_hi")
        turned_split = sem("turned_split")
        z_done = sem("z_done")
        z_hi = sem("z_hi")
        z_split = sem("z_split")
        values_done = sem("values_done")
        values_hi = sem("values_hi")
        values_split = sem("values_split")
        out_done = sem("out_done")
        out_copied = sem("out_copied")
        stats_done = sem("stats_done")
        out_stored = [sem(f"out_stored{i}") for i in range(STAGES)]

        xs = sb("xs", [P, XRING, 2, 2, HW], F32R)
        zs = sb("zs", [P, 2, 2, HW], F32R)
        vs = sb("vs", [P, 2, 2, STRIPS, C], F32R)
        ps = sb("ps", [P, 2, 2, HALF // BLOCK, STRIPS, BLOCK], F32R)
        Q = sb("Q", [P, 2, P // BLOCK, 2, STRIPS, BLOCK], F32)
        turned = sb("turned", [P, 2 * P // BLOCK, STRIPS, BLOCK], F32)
        probs = sb("probs", [P, HW], F32)
        stage = sb("stage", [P, STAGES, HALF], F32)
        mh = sb("mh", [P, 2, C], F32R)
        ml = sb("ml", [P, 2, C], F32R)
        wvh = sb("wvh", [P, 2, CW], F32R)
        wvl = sb("wvl", [P, 2, CW], F32R)
        r_bias = sb("r_bias", [P, 1], F32)
        b0_c = sb("b0_c", [P, 2], F32)
        u_c = sb("u_c", [P, 2], F32)
        b1_c = sb("b1_c", [P, 2], F32)
        b2_c = sb("b2_c", [P, 2], F32)
        ident = sb("ident", [P, P], F32)
        r_all = sb("r_all", [P, T, STRIPS], F32)
        negmax = sb("negmax", [P, 2], F32)
        shift = sb("shift", [P, 2], F32)
        total = sb("total", [P, 2], F32)
        inverse = sb("inverse", [P, 2], F32)
        xh, xl = xs[:, :, 0], xs[:, :, 1]
        zh, zl = zs[:, 0], zs[:, 1]
        vh, vl = vs[:, :, 0], vs[:, :, 1]
        ph, pl = ps[:, :, 0], ps[:, :, 1]

        sp = [psum(f"sp{i}", [P, 2, HALF]) for i in range(BUFFERS)]
        op = [psum(f"op{i}", [P, HALF]) for i in range(2)]

        FRAME = 2 * HW * 4
        homes = [("xs", 0), ("xs", 2), ("vs", 0), ("xs", 4), ("zs", 0), ("Q", 0), ("ps", 0), ("ps", 2)]
        RING = len(homes)
        ROUNDS = N // RING
        assert N % RING == 0
        pairs = [sb(f"pair{i}", [P, 2, 2, HW], F32, at=places[name] + k * FRAME) for i, (name, k) in enumerate(homes)]
        moments = sb("moments", [P, 2, 2], F32)
        varied = sb("varied", [P, 2], F32)
        root = sb("root", [P, 2], F32)
        guess = sb("guess", [P, 2], F32)
        error = sb("error", [P, 2], F32)
        gain = sb("gain", [P, 2], F32)
        offset = sb("offset", [P, 2], F32)
        chain = sem("chain")
        var_ready = sem("var_ready")
        root_ready = sem("root_ready")
        affine_ready = sem("affine_ready")
        pair_loaded = [sem(f"pair_loaded{i}") for i in range(RING)]
        pair_scaled = sem("pair_scaled")
        pair_summed = sem("pair_summed")
        pair_stored = [sem(f"pair_stored{i}") for i in range(RING)]

        w1_s, w2_s, w0_s = [sb(name, [P, 2, C], F32, at=places["Q"] + n * 2 * C * 4)
                            for n, name in enumerate(("w1_s", "w2_s", "w0_s"))]

        def strip_of(parts, k):
            blocks = parts.shape[1]
            first = k % 2 + (8 * (k // 2 % 2) if blocks == HALF // BLOCK else 0)
            return parts[:, first:first - k % 2 + 8:2].rearrange("p i j s -> p i (j s)")

        def arrival(k):
            return turned[:] if k // 2 % 2 == 0 else strips_landing[:, (k // 4) % 2]

        landing = sb("landing", [P, XRING, 2, 2, HW], F32, at=places["xs"])[:, :, 1]
        strips_landing = sb("strips_landing", list(ps.shape), F32, at=places["ps"])[:, :, 1]

        def span(a, b):
            return slice(a * P, b * P)

        with nc.Block() as block:

            @block.gpsimd
            def _(pool):
                nc.gpsimd.memset(ident[:], 0.0).then_inc(ident_zero, 1)
                pool.wait_ge(ident_zero, 1)
                nc.gpsimd.affine_select(out=ident[:], in_=ident[:], compare_op=ALU.not_equal, fill=1.0,
                                        base=0, pattern=[[-1, P]], channel_multiplier=1).then_inc(ident_ready, 1)

                def turned_lo_of(v, k):
                    half = (k // 4) % 2
                    pool.wait_ge(turned_hi, nth(v, N_STRIP, k))
                    nc.gpsimd.tensor_tensor(strip_of(pl[:, half], k), strip_of(arrival(k), k),
                                            strip_of(ph[:, half].bitcast(F32), k), ALU.subtract
                                            ).then_inc(turned_split, 1)

                for k in range(CARRY, HEAD):
                    turned_lo_of(0, k - CARRY)
                with pool.Fori(0, VIDEOS - 1) as v:
                    for k in range(HEAD, SLOTS):
                        turned_lo_of(v, k - CARRY)
                    for k in range(HEAD):
                        turned_lo_of(v + 1, k - CARRY)
                for k in range(HEAD, SLOTS + CARRY):
                    turned_lo_of(VIDEOS - 1, k - CARRY)

            @block.sync
            def _(sp_):
                for dst, src in ((w1_s, w1), (w2_s, w2)):
                    sp_.dma_start(dst[:], src.rearrange("(t p) c -> p t c", p=P)).then_inc(products_loaded, 16)
                sp_.dma_start(w0_s[:], w0.rearrange("(t p) c -> p t c", p=P)).then_inc(weights_loaded, 16)
                with nc.allow_non_contiguous_dma(reason="columns of 256 numbers"):
                    for dst, src in ((b1_c, b1), (b2_c, b2)):
                        sp_.dma_start(dst[:], src.rearrange("(t p) -> p t", p=P)).then_inc(weights_loaded, 16)
                    sp_.dma_start(landing[:, 0], x_d[0]).then_inc(x_loaded, 16)
                    for dst, src in ((b0_c, b0), (gamma_c, gamma), (beta_c, beta)):
                        sp_.dma_start(dst[:], src.rearrange("(t p) -> p t", p=P)).then_inc(columns_loaded, 16)

                def load_x(v, frame):
                    sp_.dma_start(landing[:, frame % T % XRING], x_d[v * T + frame]).then_inc(x_loaded, 16)

                def carry(v, k):
                    sp_.wait_ge(flipped, nth(v, N_STRIP, k))
                    if k // 2 % 2 == 0 and not (isinstance(v, int) and nth(v, N_STRIP, k - 4) <= 0):
                        sp_.wait_ge(turned_split, nth_by_two(v, N_STRIP, k - 4))
                    to = arrival(k)
                    base = to.shape[1] - 2 * P // BLOCK if k // 2 % 2 else 0
                    for i in range(P // BLOCK):
                        for j in range(P // BLOCK):
                            sp_.dma_start(
                                to[BLOCK * j:BLOCK * (j + 1), base + 2 * i:base + 2 * i + 2],
                                Q[BLOCK * i:BLOCK * (i + 1), k // 2 % 2, j]).then_inc(carried[k // 2 % 2], 16)

                def load_pair(n, i):
                    sp_.dma_start(pairs[i][:, 0], attended_d[n]).then_inc(pair_loaded[i], 16)
                    sp_.dma_start(pairs[i][:, 1], x_d[n]).then_inc(pair_loaded[i], 16)

                def slot(v, k, first=False, last=False, tail=False):
                    step, strip = divmod(k, STRIPS)
                    if not tail:
                        if k % 4 == 1:
                            carry(v, k)
                    _, half, m, second = out_quarter(k)
                    if second and not (first and k < LAG):
                        for frame, tile in out_tiles(k):
                            n = v * T + (frame if tile >= 0 else frame - T)
                            sp_.wait_ge(out_copied, nth(v, N_OUT, tile))
                            sp_.dma_start(attended_d[n][:, m, half * HALF:(half + 1) * HALF],
                                          stage[:, tile % STAGES, :]).then_inc(out_stored[tile % STAGES], 16)
                    if k == SLOTS - 5 and not last and not tail:
                        sp_.wait_ge(x_hi, nth(v, N_SPLIT, 2 * 7))
                        load_x(v, T)
                    if strip == STRIPS - 1 and not (last and step == STEPS - 1) and not tail:
                        sp_.wait_ge(z_done, nth(v, N_Z, 2 * (step + 1) + 1))
                        load_x(v, step + 2 if step < STEPS - 1 else T + 1)
                    if k % 4 == 3 and not tail:
                        carry(v, k)

                sp_.wait_ge(x_hi, 1)
                load_x(0, 1)
                for k in range(HEAD):
                    slot(0, k, first=True)
                with sp_.Fori(0, VIDEOS - 1) as v:
                    for k in range(HEAD, SLOTS):
                        slot(v, k)
                    for k in range(HEAD):
                        slot(v + 1, k)
                end = VIDEOS - 1
                left = {
                    STRIPS * 6: [(0, [(z_done, nth(end, N_Z, 2 * 6 + 1))])],
                    SLOTS - 2: [(1, [(values_done, nth(end, N_VAL, 4 * 7 + 3))])],
                    SLOTS: [(2, [(out_done, nth(end, N_OUT, 4 * 6 + 3))]),
                            (3, [(scores_done, VIDEOS * N_STRIP)]), (4, [])],
                    SLOTS + 3: [(5, [(c, VIDEOS * N_PAIR * CARRIED) for c in carried])],
                    SLOTS + 4: [(6, [(out_done, nth(end, N_OUT, 4 * 7 + 1))]), (7, [])],
                }
                for k in range(HEAD, SLOTS + LAG):
                    if k < SLOTS:
                        slot(end, k, last=True)
                    else:
                        slot(VIDEOS, k - SLOTS, tail=True)
                    if k == STRIPS * 6:
                        for s in out_stored:
                            sp_.wait_ge(s, 16 * end * N_OUT // STAGES)
                    for i, waits in left.get(k, []):
                        for done, count in waits:
                            sp_.wait_ge(done, count)
                        load_pair(i, i)
                for s in out_stored:
                    sp_.wait_ge(s, 16 * VIDEOS * N_OUT // STAGES)
                with sp_.Fori(1, ROUNDS) as g:
                    for i in range(RING):
                        sp_.wait_ge(pair_stored[i], 16 * g)
                        load_pair(g * RING + i, i)

            @block.tensor
            def _(pe):
                def product(outs, weights, movings, start=True, stop=True):
                    n = len(weights)
                    for c, (w_hi, w_lo) in enumerate(weights):
                        for w, part in ((w_hi, 0), (w_hi, 1), (w_lo, 0)):
                            for h, o in enumerate(outs):
                                mm = nc.tensor.matmul(o, w, movings[c][h][part],
                                                      start=start and c == 0 and part == 0 and w is w_hi,
                                                      stop=stop and c == n - 1 and w is w_lo)
                    return mm

                pe.wait_ge(products_loaded, 16 * 2)
                for i in range(2):
                    for o in range(2):
                        nc.tensor.matmul(sp[0][:, i, 0:C], w1_s[:, o, span(i, i + 1)], w2_s[:, o, :],
                                         start=o == 0, stop=o == 1)
                pe.wait_ge(weights_loaded, 16 * 3)
                pe.wait_ge(ident_ready, 1)
                for i in range(2):
                    for o in range(2):
                        nc.tensor.transpose(sp[1][:, i, span(o, o + 1)], w0_s[:, o, span(i, i + 1)], ident[:])
                for at, (w, b) in enumerate(((w2_s, b1_c), (w1_s, b2_c))):
                    for m in range(2):
                        for o in range(2):
                            nc.tensor.matmul(op[0][:, 2 * at + m:2 * at + m + 1], w[:, o, span(m, m + 1)],
                                             b[:, o:o + 1], start=o == 0, stop=o == 1)
                for o in range(2):
                    mm = nc.tensor.matmul(op[0][:, 4:5], b1_c[:, o:o + 1].to_broadcast([P, P]),
                                          b2_c[:, o:o + 1], start=o == 0, stop=o == 1)
                mm.then_inc(prep_mm, 1)

                def wait_buffer(v, unit):
                    kind, index = before_in_buffer(unit)
                    if kind == "scores":
                        if not (isinstance(v, int) and nth(v, N_STRIP, index) <= 0):
                            pe.wait_ge(exp_done, nth(v, N_STRIP, index))
                    elif kind == "z":
                        pe.wait_ge(z_split, nth(v, N_Z, index))
                    else:
                        pe.wait_ge(values_split, nth(v, N_VAL, index))

                def scores(v, k):
                    step, strip = divmod(k, STRIPS)
                    key = max(step - 1, 0) % XRING
                    wait_buffer(v, ("scores", k))
                    if strip == 0:
                        pe.wait_ge(z_split, nth(v, N_Z, 2 * step + 1))
                    a = span(strip, strip + 1)
                    halves = [slice(h * HALF, (h + 1) * HALF) for h in range(2)]
                    product([sp[BUFFER["scores", k]][:, h, :] for h in range(2)],
                            [(zh[:, c, a], zl[:, c, a]) for c in range(2)],
                            [[(xh[:, key, c, s], xl[:, key, c, s]) for s in halves] for c in range(2)]
                            ).then_inc(scores_done, 1)

                def make_z(v, frame):
                    for m in range(2):
                        index = 2 * frame + m
                        q = frame % STEPS % XRING
                        wait_buffer(v, ("z", index))
                        pe.wait_ge(x_split, nth(v, N_SPLIT, 2 * (frame if frame < STEPS else T) + 1))
                        halves = [slice(h * HALF, (h + 1) * HALF) for h in range(2)]
                        product([sp[BUFFER["z", index]][:, h, :] for h in range(2)],
                                [(mh[:, c, span(m, m + 1)], ml[:, c, span(m, m + 1)]) for c in range(2)],
                                [[(xh[:, q, c, s], xl[:, q, c, s]) for s in halves] for c in range(2)]
                                ).then_inc(z_done, 1)

                def make_values(v, indices):
                    for index in indices:
                        frame, j = divmod(index, 4)
                        q = frame % T % XRING
                        wait_buffer(v, ("values", index))
                        pe.wait_ge(x_split, nth(v, N_SPLIT, 2 * frame + 1))
                        for i in range(2):
                            a = span(2 * j + i, 2 * j + i + 1)
                            mm = product([sp[BUFFER["values", index]][:, i, 0:CW]],
                                         [(xh[:, q, c, a], xl[:, q, c, a]) for c in range(2)],
                                         [[(wvh[:, c, :], wvl[:, c, :])] for c in range(2)])
                        mm.then_inc(values_done, 1)

                def attend(v, k):
                    step, half, m, second = out_quarter(k)
                    for frame, tile in out_tiles(k):
                        if not second:
                            if m == 0:
                                pe.wait_ge(turned_split, nth(v, N_STRIP, STRIPS * step + 4 * half + 3))
                                pe.wait_ge(values_split, nth(v, N_VAL, 4 * (step + 1) + 3 if step >= 0 else -1))
                            if not (isinstance(v, int) and nth(v, N_OUT, tile - 2) <= 0):
                                pe.wait_ge(out_copied, nth(v, N_OUT, tile - 2))
                        gs = range(4 * second, 4 * second + 4)
                        mm = product([op[tile % 2][:].rearrange("p (n s) -> p n s", s=BLOCK)],
                                     [(vh[:, frame % 2, g, span(m, m + 1)], vl[:, frame % 2, g, span(m, m + 1)])
                                      for g in gs],
                                     [[(ph[:, half, :, g, :], pl[:, half, :, g, :])] for g in gs],
                                     start=not second, stop=second)
                        if second:
                            mm.then_inc(out_done, 1)

                def slot(v, k, first=False, last=False):
                    step, strip = divmod(k, STRIPS)
                    scores(v, k)
                    if strip == STRIPS - 1 and not (last and step == STEPS - 1):
                        make_z(v, step + 1)
                    if not (first and k < LAG):
                        attend(v, k)
                    make_values(v, values_of_slot(k, last))

                pe.wait_ge(prep_ready, 1)
                make_z(-1, STEPS)
                make_values(-1, values_of_slot(SLOTS - 1))
                for k in range(HEAD):
                    slot(0, k, first=True)
                with pe.Fori(0, VIDEOS - 1) as v:
                    for k in range(HEAD, SLOTS):
                        slot(v, k)
                    for k in range(HEAD):
                        slot(v + 1, k)
                for k in range(HEAD, SLOTS):
                    slot(VIDEOS - 1, k, last=True)
                for k in range(LAG):
                    attend(VIDEOS, k)

            @block.scalar
            def _(act):
                def split_x(v, frame, c):
                    q = frame % T % XRING
                    act.wait_ge(x_loaded, 16 * nth(v, T, frame))
                    nc.scalar.activation(xh[:, q, c, :], landing[:, q, c, :], ACT.Copy).then_inc(x_hi, 1)

                def values_hi_of(v, indices):
                    for index in indices:
                        frame, j = divmod(index, 4)
                        act.wait_ge(values_done, nth(v, N_VAL, index))
                        nc.scalar.activation(vh[:, frame % 2, 2 * j:2 * j + 2, :],
                                             sp[BUFFER["values", index]][:, :, 0:C],
                                             ACT.Copy).then_inc(values_hi, 1)

                def z_hi_of(v, index):
                    for m in range(2):
                        act.wait_ge(z_done, nth(v, N_Z, index + m))
                        nc.scalar.activation(zh[:, m, :], sp[BUFFER["z", index + m]][:].rearrange("p a b -> p (a b)"),
                                             ACT.Identity, bias=u_c[:, m:m + 1]).then_inc(z_hi, 1)

                def turned_hi_of(v, k):
                    act.wait_ge(carried[k // 2 % 2], CARRIED * nth(v, N_PAIR, k // 4))
                    if k % 4 == 0 and not (isinstance(v, int) and v == 0 and k + CARRY - 1 < LAG):
                        act.wait_ge(out_done, nth(v, N_OUT, out_tiles(k + CARRY - 1)[-1][1]))
                    nc.scalar.activation(strip_of(ph[:, (k // 4) % 2], k), strip_of(arrival(k), k), ACT.Copy
                                         ).then_inc(turned_hi, 1)

                def copy_out(v, k):
                    _, _, m, second = out_quarter(k)
                    if second:
                        for _, tile in out_tiles(k):
                            act.wait_ge(out_done, nth(v, N_OUT, tile))
                            if not (isinstance(v, int) and nth(v, N_OUT, tile - STAGES) <= 0):
                                act.wait_ge(out_stored[tile % STAGES],
                                            16 * (v * (N_OUT // STAGES) + (tile - tile % STAGES) // STAGES))
                                act.wait_ge(stats_done, nth(v, N_OUT, tile - STAGES))
                            for r in range(2):
                                copy = nc.scalar.activation(
                                    stage[:, tile % STAGES, span(2 * r, 2 * r + 2)].rearrange(
                                        "p (k i s) -> p i k s", k=2, s=BLOCK),
                                    op[tile % 2][:, span(2 * r, 2 * r + 2)].rearrange(
                                        "p (i k s) -> p i k s", k=2, s=BLOCK),
                                    ACT.Identity, bias=b0_c[:, m:m + 1])
                            copy.then_inc(out_copied, 1)

                def slot(v, k, first=False, last=False):
                    step, strip = divmod(k, STRIPS)
                    act.wait_ge(shift_done, nth(v, N_STRIP, k))
                    if not (first and k < 1):
                        act.wait_ge(flipped, nth(v, N_STRIP, k - 1))
                    nc.scalar.activation(probs[:], sp[BUFFER["scores", k]][:].rearrange("p a b -> p (a b)"),
                                         ACT.Exp, bias=shift[:, k % 2:k % 2 + 1],
                                         accum_out=total[:, k % 2:k % 2 + 1]).then_inc(exp_done, 1)
                    if strip == STRIPS - 1 and not (last and step == STEPS - 1):
                        z_hi_of(v, 2 * (step + 1))
                    if k % 4 == 2 and not (first and k < CARRY):
                        turned_hi_of(v, k - CARRY)
                        turned_hi_of(v, k - CARRY + 1)
                    if not (first and k < LAG):
                        copy_out(v, k)
                    values_hi_of(v, values_of_slot(k, last))
                    if k % 4 == 0 and not (first and k < CARRY):
                        turned_hi_of(v, k - CARRY)
                        turned_hi_of(v, k - CARRY + 1)
                    if strip in (1, 2):
                        split_x(v, step + 1, strip - 1)
                    if k in (SLOTS - 3, SLOTS - 2) and not last:
                        split_x(v, T, k - (SLOTS - 3))

                for c in range(2):
                    split_x(0, 0, c)
                act.wait_ge(prep_mm, 1)
                nc.scalar.activation(mh[:], sp[0][:, :, 0:C], ACT.Copy, scale=SCALE).then_inc(prep_hi, 1)
                nc.scalar.activation(wvh[:, :, 0:C], sp[1][:, :, 0:C], ACT.Copy).then_inc(prep_hi, 1)
                z_hi_of(-1, 2 * STEPS)
                values_hi_of(-1, values_of_slot(SLOTS - 1))
                act.wait_ge(columns_loaded, 16 * 3)
                for k in range(HEAD):
                    slot(0, k, first=True)
                with act.Fori(0, VIDEOS - 1) as v:
                    for k in range(HEAD, SLOTS):
                        slot(v, k)
                    for k in range(HEAD):
                        slot(v + 1, k)
                for k in range(HEAD, SLOTS):
                    slot(VIDEOS - 1, k, last=True)
                for k in range(LAG):
                    if k < CARRY and k % 2 == 0:
                        turned_hi_of(VIDEOS, k - CARRY)
                        turned_hi_of(VIDEOS, k - CARRY + 1)
                    copy_out(VIDEOS, k)

                act.wait_ge(var_ready, 1)
                nc.scalar.activation(root[:], varied[:], ACT.Sqrt).then_inc(root_ready, 1)
                act.wait_ge(affine_ready, 1)

                def scale(n, i, g):
                    act.wait_ge(pair_loaded[i], 32 * (g + 1))
                    for c in range(2):
                        nc.scalar.activation(pairs[i][:, 0, c, :], pairs[i][:, 0, c, :], ACT.Identity,
                                             bias=offset[:, c:c + 1], scale=gain[:, c:c + 1]).then_inc(pair_scaled, 1)

                def store(n, i):
                    act.wait_ge(pair_summed, 2 * (n + 1))
                    act.dma_start(out_d[n], pairs[i][:, 0]).then_inc(pair_stored[i], 16)

                scale(0, 0, 0)
                for i in range(1, RING):
                    scale(i, i, 0)
                    store(i - 1, i - 1)
                with act.Fori(1, ROUNDS) as g:
                    for i in range(RING):
                        store(g * RING + i - 1, (i - 1) % RING)
                        scale(g * RING + i, i, g)
                store(N - 1, RING - 1)
                for i in range(RING):
                    act.wait_ge(pair_stored[i], 16 * ROUNDS)

            @block.vector
            def _(dve):
                nc.vector.memset(wvh[:, :, CW - 1:CW].bitcast(F32), 0.0)
                nc.vector.memset(wvl[:, :, CW - 1:CW].bitcast(F32), 0.0)

                def split_x(v, frame, c):
                    q = frame % T % XRING
                    dve.wait_ge(x_hi, nth(v, N_SPLIT, 2 * frame + c))
                    nc.vector.tensor_tensor(xl[:, q, c, :], landing[:, q, c, :], xh[:, q, c, :].bitcast(F32),
                                            ALU.subtract).then_inc(x_split, 1)

                def values_lo_of(v, indices):
                    for index in indices:
                        frame, j = divmod(index, 4)
                        values = sp[BUFFER["values", index]]
                        dve.wait_ge(values_hi, nth(v, N_VAL, index))
                        nc.vector.tensor_scalar(r_all[:, frame % T, 2 * j:2 * j + 2], values[:, :, C], r_bias[:], None,
                                                ALU.add)
                        nc.vector.tensor_tensor(vl[:, frame % 2, 2 * j:2 * j + 2, :], values[:, :, 0:C],
                                                vh[:, frame % 2, 2 * j:2 * j + 2, :].bitcast(F32),
                                                ALU.subtract).then_inc(values_split, 1)

                def z_lo_of(v, index):
                    for m in range(2):
                        dve.wait_ge(z_hi, nth(v, N_Z, index + m))
                        nc.vector.scalar_tensor_tensor(
                            out=zl[:, m, :], in0=sp[BUFFER["z", index + m]][:].rearrange("p a b -> p (a b)"),
                            scalar=u_c[:, m:m + 1], in1=zh[:, m, :].bitcast(F32), op0=ALU.add,
                            op1=ALU.subtract).then_inc(z_split, 1)

                def statistics(v, k):
                    _, half, m, second = out_quarter(k)
                    if second:
                        for frame, tile in out_tiles(k):
                            n = (v * T + (frame if tile >= 0 else frame - T)) * 2 + half
                            dve.wait_ge(out_copied, nth(v, N_OUT, tile))
                            nc.vector.bn_stats(stats[:, m, n, :], stage[:, tile % STAGES, :]).then_inc(stats_done, 1)

                def slot(v, k, first=False, last=False):
                    step, strip = divmod(k, STRIPS)
                    two = slice(k % 2, k % 2 + 1)
                    r = r_all[:, step, strip:strip + 1]
                    dve.wait_ge(scores_done, nth(v, N_STRIP, k))
                    nc.vector.tensor_reduce(negmax[:, two], sp[BUFFER["scores", k]][:].rearrange("p a b -> p (a b)"),
                                            AX_X, ALU.max, negate=True).then_inc(max_done, 1)
                    if strip == 0:
                        dve.wait_ge(values_split, nth(v, N_VAL, 4 * step + 3))
                    dve.wait_ge(max_done, nth(v, N_STRIP, k))
                    nc.vector.scalar_tensor_tensor(out=shift[:, two], in0=negmax[:, two], scalar=r, in1=r,
                                                   op0=ALU.subtract, op1=ALU.add).then_inc(shift_done, 1)
                    dve.wait_ge(exp_done, nth(v, N_STRIP, k))
                    nc.vector.reciprocal(inverse[:, two], total[:, two]).then_inc(recip_done, 1)
                    dve.wait_ge(recip_done, nth(v, N_STRIP, k))
                    nc.vector.tensor_scalar(probs[:], probs[:], inverse[:, two], None, ALU.mult).then_inc(probs_done, 1)
                    dve.wait_ge(probs_done, nth(v, N_STRIP, k))
                    if not (isinstance(v, int) and nth(v, N_PAIR, k // 4 - 1) <= 0):
                        dve.wait_ge(carried[k // 2 % 2], CARRIED * nth(v, N_PAIR, k // 4 - 1))
                    nc.vector.transpose(Q[:, k // 2 % 2, :, k % 2].rearrange("p jj j s -> p j jj s"), probs[:]
                                        ).then_inc(flipped, 1)
                    if strip == STRIPS - 1 and not (last and step == STEPS - 1):
                        z_lo_of(v, 2 * (step + 1))
                    if not (first and k < LAG):
                        statistics(v, k)
                    values_lo_of(v, values_of_slot(k, last))
                    if strip in (1, 2):
                        split_x(v, step + 1, strip - 1)
                    if k in (SLOTS - 3, SLOTS - 2) and not last:
                        split_x(v, T, k - (SLOTS - 3))

                for c in range(2):
                    split_x(0, 0, c)
                dve.wait_ge(prep_mm, 1)
                nc.vector.tensor_scalar(u_c[:], op[0][:, 0:2], SCALE, None, ALU.mult)
                nc.vector.tensor_scalar(r_bias[:], op[0][:, 4:5], SCALE, None, ALU.mult)
                for j in range(2):
                    nc.vector.tensor_scalar(wvh[:, j, C:C + 1], op[0][:, 2 + j:3 + j], SCALE, None, ALU.mult
                                            ).then_inc(prep_hi, 1)
                dve.wait_ge(prep_hi, 4)
                for j in range(2):
                    nc.vector.scalar_tensor_tensor(out=wvl[:, j, C:C + 1], in0=op[0][:, 2 + j:3 + j], scalar=SCALE,
                                                   in1=wvh[:, j, C:C + 1].bitcast(F32), op0=ALU.mult, op1=ALU.subtract)
                nc.vector.scalar_tensor_tensor(out=ml[:], in0=sp[0][:, :, 0:C], scalar=SCALE, in1=mh[:].bitcast(F32),
                                               op0=ALU.mult, op1=ALU.subtract)
                nc.vector.tensor_tensor(wvl[:, :, 0:C], sp[1][:, :, 0:C], wvh[:, :, 0:C].bitcast(F32),
                                        ALU.subtract).then_inc(prep_ready, 1)
                z_lo_of(-1, 2 * STEPS)
                values_lo_of(-1, values_of_slot(SLOTS - 1))
                for k in range(HEAD):
                    slot(0, k, first=True)
                with dve.Fori(0, VIDEOS - 1) as v:
                    for k in range(HEAD, SLOTS):
                        slot(v, k)
                    for k in range(HEAD):
                        slot(v + 1, k)
                for k in range(HEAD, SLOTS):
                    slot(VIDEOS - 1, k, last=True)
                for k in range(LAG):
                    statistics(VIDEOS, k)

                links = [0]

                def link(ins):
                    links[0] += 1
                    ins.then_inc(chain, 1)
                    dve.wait_ge(chain, links[0])

                dve.wait_ge(columns_loaded, 16 * 3)
                dve.wait_ge(stats_done, VIDEOS * N_OUT)
                for c in range(2):
                    link(nc.vector.bn_aggr(moments[:, c, :], stats[:, c, :, :].rearrange("p n s -> p (n s)")))
                nc.vector.tensor_scalar(varied[:], moments[:, :, 1], EPS, None, ALU.add).then_inc(var_ready, 1)
                dve.wait_ge(root_ready, 1)
                link(nc.vector.reciprocal(guess[:], root[:]))
                for _ in range(2):
                    link(nc.vector.tensor_tensor(error[:], guess[:], guess[:], ALU.mult))
                    link(nc.vector.tensor_tensor(error[:], error[:], varied[:], ALU.mult))
                    link(nc.vector.tensor_scalar(error[:], error[:], -0.5, 1.5, ALU.mult, ALU.add))
                    link(nc.vector.tensor_tensor(guess[:], guess[:], error[:], ALU.mult))
                link(nc.vector.tensor_tensor(gain[:], guess[:], gamma_c[:], ALU.mult))
                link(nc.vector.tensor_tensor(error[:], gain[:], moments[:, :, 0], ALU.mult))
                nc.vector.tensor_tensor(offset[:], beta_c[:], error[:], ALU.subtract).then_inc(affine_ready, 1)

                with dve.Fori(0, ROUNDS) as g:
                    for i in range(RING):
                        for c in range(2):
                            dve.wait_ge(pair_scaled, 2 * (g * RING + i) + c + 1)
                            nc.vector.tensor_tensor(pairs[i][:, 0, c, :], pairs[i][:, 0, c, :], pairs[i][:, 1, c, :],
                                                    ALU.add).then_inc(pair_summed, 1)

_INS = ["x", "L0_conv_w1", "L0_conv_b1", "L0_conv_w2", "L0_conv_b2", "L0_conv_w0", "L0_conv_b0", "L0_conv_gamma",
        "L0_conv_beta"]


def kernel(**inputs):
    import numpy as _np
    import concourse.bacc as _bacc
    from concourse import mybir as _mybir
    from concourse.bass_utils import run_bass_kernel_spmd as _run

    nc = _bacc.Bacc("TRN2", target_bir_lowering=False, num_devices=1)
    arrays, args = {}, []
    for name in _INS:
        a = _np.ascontiguousarray(inputs[name])
        arrays[f"in_{name}_dram"] = a
        args.append(nc.dram_tensor(f"in_{name}_dram", a.shape, _mybir.dt.from_np(a.dtype), kind="ExternalInput").ap())
    y = nc.dram_tensor("out_0_dram", inputs["x"].shape, _mybir.dt.float32, kind="ExternalOutput").ap()
    conv_attention_norm(nc, *args, y)
    r = _run(nc, [arrays], core_ids=[0])
    return r.results[0]["out_0_dram"]
```
